# Optimizing a Trainium2 kernel written in Bass

```python
import numpy as np
import jax
import jax.numpy as jnp

def _softmax(x, axis=-1):
    return jax.nn.softmax(x, axis=axis)

def _gelu(x):
    return jax.nn.gelu(x, approximate=True)

def _silu(x):
    return jax.nn.silu(x)

def _sigmoid(x):
    return jax.nn.sigmoid(x)

def _layernorm(x, axis=-1, eps=1e-05):
    m = jnp.mean(x, axis=axis, keepdims=True)
    v = jnp.var(x, axis=axis, keepdims=True)
    return (x - m) / jnp.sqrt(v + eps)

def _scatter_add(tgt, idx, src, axis=0):
    return tgt.at[idx].add(src)

def _segment_sum(src, seg, n):
    return jax.ops.segment_sum(src, seg, n)
kernel_name = 'mk_gnn_resnorm_d2_gnn_r64_2f5480'

def setup_inputs(seed: int=0):
    np.random.seed(seed)
    _w = jnp.asarray

    def _rec_inputs():
        import jax
        import jax.numpy as jnp
        _gk = jax.random.key(seed)
        x = -0.0008691 + 1 * jax.random.normal(jax.random.fold_in(_gk, 1), (50000, 128), jnp.float32)
        src = jax.random.randint(jax.random.fold_in(_gk, 2), (12500,), 0, 50000, jnp.int32)
        dst = jax.random.randint(jax.random.fold_in(_gk, 3), (12500,), 0, 50000, jnp.int32)
        _o = jnp.argsort(dst, stable=True)
        src = src[_o]
        dst = dst[_o]
        edge_attr_128 = -8.513e-05 + 0.999844 * jax.random.normal(jax.random.fold_in(_gk, 12), (12500, 128), jnp.float32)
        edge_type_8 = jax.random.randint(jax.random.fold_in(_gk, 14), (12500,), 0, 8, jnp.int32)
        return (x, src, dst, edge_attr_128, edge_type_8)
    x, src, dst, edge_attr_128, edge_type_8 = _rec_inputs()

    def _L0_gnn_setup():
        import jax, jax.numpy as jnp
        import numpy as np
        N_NODES = 10000
        N_EDGES = 10000
        D = 128
        key = jax.random.key(seed)
        ks = jax.random.split(key, 10)
        sc = 1.0 / np.sqrt(D)
        return {'node_features': jax.random.normal(ks[0], (N_NODES, D), jnp.float32), 'edge_features': jax.random.normal(ks[1], (N_EDGES, D), jnp.float32), 'src': jax.random.randint(ks[2], (N_EDGES,), 0, N_NODES), 'dst': jax.random.randint(ks[3], (N_EDGES,), 0, N_NODES), 'W_node': jax.random.normal(ks[4], (D, D), jnp.float32) * sc, 'b_node': jnp.zeros((D,), jnp.float32), 'W_edge': jax.random.normal(ks[5], (D, D), jnp.float32) * sc, 'b_edge': jnp.zeros((D,), jnp.float32), 'W_msg': jax.random.normal(ks[6], (D, D), jnp.float32) * sc, 'b_msg': jnp.zeros((D,), jnp.float32)}
    _L0_gnn_all = _L0_gnn_setup()
    _L0_gnn_in = {k: v for k, v in _L0_gnn_all.items() if k in ('W_node', 'b_node', 'W_edge', 'b_edge', 'W_msg', 'b_msg')}
    del _L0_gnn_all

    def _L1_gnn_setup():
        import jax, jax.numpy as jnp
        import numpy as np
        N_NODES = 50000
        N_EDGES = 500000
        F_DIM = 128
        N_REL = 8
        N_LAYERS = 2
        NEG_SLOPE = 0.2

        def _segment_softmax(logits, seg, num_segments):
            m = jax.ops.segment_max(logits, seg, num_segments=num_segments)
            m = jax.lax.stop_gradient(m)
            e = jnp.exp(logits - m[seg])
            denom = jax.ops.segment_sum(e, seg, num_segments=num_segments)
            return e / (denom[seg] + 1e-16)

        def _rgat_layer(h, src, dst, edge_type, W, q, k, b):
            n = h.shape[0]
            xw = jnp.einsum('nf,rfg->rng', h, W)
            out_j = xw[edge_type, src]
            out_i = xw[edge_type, dst]
            logits = jax.nn.leaky_relu((out_i @ q + out_j @ k)[:, 0], NEG_SLOPE)
            alpha = _segment_softmax(logits, dst, n)
            agg = jax.ops.segment_sum(alpha[:, None] * out_j, dst, num_segments=n)
            return agg + b
        key = jax.random.key(seed)
        ks = jax.random.split(key, 6)
        x = jax.random.normal(ks[0], (N_NODES, F_DIM), dtype=jnp.float32)
        edge_index = jax.random.randint(ks[1], (2, N_EDGES), 0, N_NODES)
        edge_type = jax.random.randint(ks[2], (N_EDGES,), 0, N_REL)
        W = jax.random.normal(ks[3], (N_LAYERS, N_REL, F_DIM, F_DIM), dtype=jnp.float32) * (1.0 / np.sqrt(F_DIM)).astype(np.float32)
        att_q = jax.random.normal(ks[4], (N_LAYERS, F_DIM, 1), dtype=jnp.float32) * 0.1
        att_k = jax.random.normal(ks[5], (N_LAYERS, F_DIM, 1), dtype=jnp.float32) * 0.1
        bias = jnp.zeros((N_LAYERS, F_DIM), dtype=jnp.float32)
        return {'x': x, 'W': W, 'att_q': att_q, 'att_k': att_k, 'bias': bias, 'edge_index': edge_index, 'edge_type': edge_type}
    _L1_gnn_all = _L1_gnn_setup()
    _L1_gnn_in = {k: v for k, v in _L1_gnn_all.items() if k in ('W', 'att_q', 'att_k', 'bias')}
    del _L1_gnn_all
    return {'x': x, 'src': src, 'dst': dst, 'edge_attr_128': edge_attr_128, 'edge_type_8': edge_type_8, 'L0_gnn_W_node': _L0_gnn_in['W_node'], 'L0_gnn_b_node': _L0_gnn_in['b_node'], 'L0_gnn_W_edge': _L0_gnn_in['W_edge'], 'L0_gnn_b_edge': _L0_gnn_in['b_edge'], 'L0_gnn_W_msg': _L0_gnn_in['W_msg'], 'L0_gnn_b_msg': _L0_gnn_in['b_msg'], 'L1_gnn_W': _L1_gnn_in['W'], 'L1_gnn_att_q': _L1_gnn_in['att_q'], 'L1_gnn_att_k': _L1_gnn_in['att_k'], 'L1_gnn_bias': _L1_gnn_in['bias']}

def reference(x, src, dst, edge_attr_128, edge_type_8, L0_gnn_W_node, L0_gnn_b_node, L0_gnn_W_edge, L0_gnn_b_edge, L0_gnn_W_msg, L0_gnn_b_msg, L1_gnn_W, L1_gnn_att_q, L1_gnn_att_k, L1_gnn_bias):
    import jax
    import jax.numpy as jnp

    def _L0_gnn_ref(node_features, edge_features, src, dst, W_node, b_node, W_edge, b_edge, W_msg, b_msg):
        import jax, jax.numpy as jnp
        import numpy as np
        N_NODES = 10000
        N_EDGES = 10000
        D = 128
        h = node_features @ W_node.T + b_node
        e = edge_features @ W_edge.T + b_edge
        msg = h[src] + e
        msg = msg @ W_msg.T + b_msg
        n = node_features.shape[0]
        s = jax.ops.segment_sum(msg, dst, num_segments=n)
        deg = jax.ops.segment_sum(jnp.ones(dst.shape, msg.dtype), dst, num_segments=n)
        return s / jnp.maximum(deg, 1.0)[:, None]

    def _L1_gnn_ref(x, W, att_q, att_k, bias, edge_index, edge_type):
        import jax, jax.numpy as jnp
        import numpy as np
        N_NODES = 50000
        N_EDGES = 500000
        F_DIM = 128
        N_REL = 8
        N_LAYERS = 2
        NEG_SLOPE = 0.2

        def _segment_softmax(logits, seg, num_segments):
            m = jax.ops.segment_max(logits, seg, num_segments=num_segments)
            m = jax.lax.stop_gradient(m)
            e = jnp.exp(logits - m[seg])
            denom = jax.ops.segment_sum(e, seg, num_segments=num_segments)
            return e / (denom[seg] + 1e-16)

        def _rgat_layer(h, src, dst, edge_type, W, q, k, b):
            n = h.shape[0]
            xw = jnp.einsum('nf,rfg->rng', h, W)
            out_j = xw[edge_type, src]
            out_i = xw[edge_type, dst]
            logits = jax.nn.leaky_relu((out_i @ q + out_j @ k)[:, 0], NEG_SLOPE)
            alpha = _segment_softmax(logits, dst, n)
            agg = jax.ops.segment_sum(alpha[:, None] * out_j, dst, num_segments=n)
            return agg + b
        src, dst = (edge_index[0], edge_index[1])
        h = x
        for l in range(W.shape[0]):
            h = _rgat_layer(h, src, dst, edge_type, W[l], att_q[l], att_k[l], bias[l])
            h = jax.nn.relu(h)
        return h
    edge_index = jnp.stack([src, dst])
    x = _layernorm(x + _L0_gnn_ref(x, edge_attr_128, src, dst, L0_gnn_W_node, L0_gnn_b_node, L0_gnn_W_edge, L0_gnn_b_edge, L0_gnn_W_msg, L0_gnn_b_msg), axis=-1)
    x = _layernorm(x + _L1_gnn_ref(x, L1_gnn_W, L1_gnn_att_q, L1_gnn_att_k, L1_gnn_bias, edge_index, edge_type_8), axis=-1)
    return x

_drawn_inputs = setup_inputs


def setup_inputs(seed=0):
    import zlib

    import numpy as np

    out = dict(_drawn_inputs(seed))
    spreads = {'L0_gnn_b_node': (0.0, 0.293),
     'L0_gnn_b_edge': (0.0, 0.289),
     'L0_gnn_b_msg': (0.0, 0.268),
     'L1_gnn_bias': (0.0, 0.1)}
    factors = {'L1_gnn_att_q': 51.166, 'L1_gnn_att_k': 45.233}
    for name, (base, spread) in spreads.items():
        noise = np.random.default_rng([zlib.crc32(name.encode()), seed]).standard_normal(out[name].shape)
        drawn = base * np.exp(spread * noise) if base else spread * noise
        out[name] = jnp.asarray(drawn.astype(out[name].dtype))
    for name, factor in factors.items():
        out[name] = (out[name] * factor).astype(out[name].dtype)
    return out
```

```python
from contextlib import ExitStack

import concourse.bass as bass
from concourse import mybir

ALU = mybir.AluOpType
ACT = mybir.ActivationFunctionType
AX = mybir.AxisListType
F32 = mybir.dt.float32
BF16 = mybir.dt.bfloat16
I32 = mybir.dt.int32
U8 = mybir.dt.uint8

P = 128
EPS = 1e-5
SLOPE = 0.2
BIG = 1.0e30
SKIP = 1.0e6
G = 7
LOOP_A, LOOP_P, LOOP_F0, LOOP_F = 174, 10, 52, (26, 54)


class Tally:

    def __init__(self, eng, sem):
        self.eng, self.sem, self.base, self.turn, self.per, self.k = eng, sem, 0, None, 0, 0

    def of(self, ins):
        ins.then_inc(self.sem, 1)
        self.k += 1
        return ins

    def wait(self):
        n = self.base + self.k
        self.eng.wait_ge(self.sem, n if self.turn is None else self.turn * self.per + n)

    def step(self, ins):
        self.of(ins)
        self.wait()

    def enter(self, turn, per):
        self.base, self.k, self.turn, self.per = self.base + self.k, 0, turn, per

    def leave(self, turns):
        assert self.k == self.per, (self.k, self.per)
        self.base, self.k, self.turn = self.base + self.per * turns, 0, None


def graph_layers(nc, x, src, dst, ea, typ, w_node, b_node, w_edge, b_edge, w_msg, b_msg, w_rel, att_q,
                 att_k, bias, out):
    N, D = x.shape
    E = src.shape[0]
    R = w_rel.shape[1]
    TL = -(-E // P)
    TL += -TL % G
    NG = TL // G
    EP = P * TL
    FULL = E // TL
    REST = E - FULL * TL
    assert D == P and FULL == P - 1 and 0 < REST < TL and TL <= P
    BR = 6
    BC = N // P // BR
    BREM = N - BC * BR * P
    assert BREM <= P and (N // P) % BR == 0
    SLOTS = 4
    GD = G * D

    x1_table = nc.dram_tensor("x1_table", (EP, D), F32).ap()
    h1_table = nc.dram_tensor("h1_table", (EP, D), F32).ap()
    src_cols = nc.dram_tensor("src_cols", (TL, P), F32).ap()
    typ_cols = nc.dram_tensor("typ_cols", (TL, P), U8).ap()

    with ExitStack() as ctx:
        def sb(name, shape, dt=F32):
            return ctx.enter_context(nc.sbuf_tensor(name, shape, dt))

        def sem(name):
            return ctx.enter_context(nc.semaphore(name))

        xs = sb("xs", [P, TL, D])
        ysz = sb("ysz", [P, TL + 1, D])
        xd = sb("xd", [P, TL, D])
        work = sb("work", [P, 2, GD])
        stage = sb("stage", [P, SLOTS * BR * D + 64])
        opT = sb("opT", [P, 2, GD])
        typB = sb("typB", [P, TL, P], U8)
        wr = sb("wr", [P, R, D])
        identS = sb("identS", [P, P + 2])
        ones = sb("ones", [P, P])
        sel0 = sb("sel0", [P, P])
        carryF = sb("carryF", [P, P])
        carryB = sb("carryB", [P, P])
        m_node = sb("m_node", [P, P])
        m_edge = sb("m_edge", [P, P])
        c_row = sb("c_row", [P, P])
        bias_row = sb("bias_row", [P, 2, P])
        relu_row = sb("relu_row", [P, 2, P])
        carry = sb("carry", [P, P])
        turn = sb("turn", [P, P + 1])
        far = sb("far", [P, P])
        wqk = sb("wqk", [P, 2, R, 2])
        qk = sb("qk", [P, 2, 2])
        bcol = sb("bcol", [P, 4])
        tick = sb("tick", [P, 1])
        first = sb("first", [P, 1])
        epsc = sb("epsc", [P, 1])
        srcI = sb("srcI", [P, TL], I32)
        dstI = sb("dstI", [P, TL], I32)
        dstG = sb("dstG", [P, TL], I32)
        outI = sb("outI", [P, TL], I32)
        posI = sb("posI", [P, TL], I32)
        cols = {n: sb("c_" + n, [P, TL]) for n in
                ("same", "next", "pre", "suf", "rcp", "typ", "src1", "lg", "fm", "m", "t0")}
        colbf = sb("colbf", [P, 2, TL + 1], BF16)
        st = sb("st", [P, 2, 2 * BR, 6])
        sm = sb("sm", [P, 2, 2 * BR, 2])
        df = sb("df", [P, 2, 2 * BR])
        sd = sb("sd", [P, 2, 2 * BR])
        rs = sb("rs", [P, 2, 2 * BR])
        nm = sb("nm", [P, 2, 2 * BR])
        st7 = sb("st7", [P, G, 6])
        sm7 = sb("sm7", [P, G, 2])
        df7 = sb("df7", [P, G])
        sd7 = sb("sd7", [P, G])
        rs7 = sb("rs7", [P, 2, G])
        nm7 = sb("nm7", [P, 2, G])

        ps_y = ctx.enter_context(nc.psum_tensor("ps_y", [P, 2, 1024], F32))
        ps_t = ctx.enter_context(nc.psum_tensor("ps_t", [P, 1024], F32))
        ps_k = ctx.enter_context(nc.psum_tensor("ps_k", [P, 512], F32))
        ps_s = ctx.enter_context(nc.psum_tensor("ps_s", [P, 512], F32))

        ident = identS[:, 1:P + 1]
        ys = ysz[:, 1:TL + 1, :]
        same, nxt, pre, suf, rcp = (cols[n] for n in ("same", "next", "pre", "suf", "rcp"))
        typF, src1, lg, fm, mx, t0 = (cols[n] for n in ("typ", "src1", "lg", "fm", "m", "t0"))
        scr = xd[:, 0:16, :].rearrange("p a b -> p (a b)")
        prevI, nextI, typI, aboveI, diffI, lowI, dstF, srcF = (
            scr[:, j * P:j * P + TL].bitcast(I32) if j < 6 else scr[:, j * P:j * P + TL] for j in range(8))
        diags = scr[:, 8 * P:10 * P]
        spread = xd[:, 52:55, :].rearrange("p a b -> p (a b)")
        w_sm = scr[:, 10 * P:13 * P].rearrange("p (a b) -> p a b", a=3)
        w_mT = scr[:, 13 * P:14 * P]
        b_rep = scr[:, 14 * P:15 * P]
        bm_row = scr[:, 15 * P:16 * P]
        colsT = xd[:, 16:18, :].rearrange("p a b -> p (a b)")
        typT8 = xd[:, 18, 0:P // 4].bitcast(U8)
        wT = xd[:, 20:36, :]
        w_all = xd[:, 36:52, :]
        k8 = stage[:, 0:TL * R].rearrange("p (t r) -> p t r", r=R)
        q8 = stage[:, TL * R:2 * TL * R].rearrange("p (t r) -> p t r", r=R)
        hot = stage[:, 2 * TL * R:3 * TL * R].rearrange("p (t r) -> p t r", r=R)
        tmp8 = stage[:, 3 * TL * R:4 * TL * R].rearrange("p (t r) -> p t r", r=R)
        posw = stage[:, 0:G * TL].rearrange("p (t r) -> p t r", r=TL)
        posn = stage[:, G * TL:(G + 1) * TL]
        post = stage[:, (G + 1) * TL:(G + 2) * TL]
        stepT = opT[:].bitcast(BF16)

        def slot(c):
            b = c % SLOTS
            return stage[:, b * BR * D:(b + 1) * BR * D].rearrange("p (r d) -> p r d", d=D)

        def grp(t, g):
            return t[:, bass.ds(g * G, G), :] if not isinstance(g, int) else t[:, g * G:g * G + G, :]

        def grpc(t, g):
            return t[:, bass.ds(g * G, G)] if not isinstance(g, int) else t[:, g * G:g * G + G]

        def row_of(t, c):
            return t[:, bass.ds(c, 1), :].rearrange("p a d -> p (a d)") if not isinstance(c, int) else t[:, c, :]

        def at(t, c):
            return t[:, bass.ds(c, 1)] if not isinstance(c, int) else t[:, c:c + 1]

        def wide(ap, n):
            return ap.unsqueeze(2).to_broadcast([ap.shape[0], ap.shape[1], n])

        def mid(ap, n):
            return ap.unsqueeze(1).to_broadcast([ap.shape[0], n, ap.shape[1]])

        idx_in = sem("idx_in"); par_in = sem("par_in"); ea_in = sem("ea_in"); w0_in = sem("w0_in"); w1_in = sem("w1_in")
        cols_out = sem("cols_out"); typB_in = sem("typB_in"); srcB_in = [sem(f"srcB_in{u}") for u in range(2)]
        bulk_in = [sem(f"bulk_in{b}") for b in range(SLOTS)]
        bulk_out = [sem(f"bulk_out{b}") for b in range(SLOTS)]
        xs_in = [[sem(f"xs_in{j}{u}") for u in range(2)] for j in range(3)]
        xd_in = [sem(f"xd_in{u}") for u in range(2)]
        tab_out = [[sem(f"tab_out{j}{u}") for u in range(2)] for j in range(2)]
        rows_out = sem("rows_out")
        consts = sem("consts"); fills = sem("fills"); idx_f = sem("idx_f"); idx_T = sem("idx_T"); idx_Tsb = sem("idx_Tsb")
        diag_r = sem("diag_r"); diag_p = sem("diag_p")
        wmT_p = sem("wmT_p"); wmT_s = sem("wmT_s"); wrT_p = sem("wrT_p"); wrT_s = sem("wrT_s")
        brep_r = sem("brep_r"); mix_p = sem("mix_p"); mix_s = sem("mix_s"); c_r = sem("c_r"); wqk_p = sem("wqk_p"); wqk_s = sem("wqk_s")
        prol_d = sem("prol_d")
        pro = sem("dve_steps")
        b_sum = sem("b_sum"); b_sd = sem("b_sd"); b_rs = sem("b_rs"); b_norm1 = sem("b_norm1"); b_norm2 = sem("b_norm2")
        a_T = sem("a_T"); a_Ts = sem("a_Ts"); a_msg = sem("a_msg"); a_ys = sem("a_ys")
        a_sum = sem("a_sum"); a_sd = sem("a_sd"); a_rs = sem("a_rs"); a_norm = sem("a_norm"); a_scan = sem("a_scan")
        p_step = sem("p_step"); p_row = sem("p_row"); p_ready = sem("p_ready")
        cy_in = sem("cy_in"); cy_ps = sem("cy_ps")
        f_sum = [sem(f"f_sum{j}") for j in range(3)]; f_sd = [sem(f"f_sd{j}") for j in range(3)]
        f_rs = [sem(f"f_rs{j}") for j in range(3)]; f_rows = [sem(f"f_rows{j}") for j in range(3)]
        f_T = [sem(f"f_T{j}") for j in range(2)]; f_Ts = [sem(f"f_Ts{j}") for j in range(2)]
        f_q = [sem(f"f_q{j}") for j in range(2)]; f_qs = [sem(f"f_qs{j}") for j in range(2)]
        m_T = [sem(f"m_T{j}") for j in range(2)]; m_Ts = [sem(f"m_Ts{j}") for j in range(2)]
        m_k = [sem(f"m_k{j}") for j in range(2)]; m_ks = [sem(f"m_ks{j}") for j in range(2)]
        m_mask = [sem(f"m_mask{j}") for j in range(2)]; m_used = [sem(f"m_used{j}") for j in range(2)]
        m_ys = [sem(f"m_ys{j}") for j in range(2)]
        s_arg = [sem(f"s_arg{j}") for j in range(2)]; s_exp = [sem(f"s_exp{j}") for j in range(2)]
        n_y = [sem(f"n_y{j}") for j in range(2)]
        refill = sem("refill")

        x_bulk = x[0:BC * BR * P].rearrange("(p r) d -> p r d", p=P)
        o_bulk = out[0:BC * BR * P].rearrange("(p r) d -> p r d", p=P)
        x1_rows = x1_table.rearrange("(p t) d -> p t d", p=P)
        h1_rows = h1_table.rearrange("(p t) d -> p t d", p=P)
        tables = [(x1_table, x1_rows), (h1_table, h1_rows)]

        def flat(v, a, n):
            return v[a:a + n]

        def load_cols(eng, dest, v, s):
            eng.dma_start(dest[0:FULL, :], v[0:FULL * TL].rearrange("(p t) -> p t", t=TL)).then_inc(s, 16)
            eng.dma_start(dest[FULL:P, 0:REST], v[FULL * TL:E].rearrange("(a t) -> a t", a=1)).then_inc(s, 16)

        N_IDX = 14
        N_PAR = 13

        block = ctx.enter_context(nc.Block())

        @block.sync
        def _(sp):
            load_cols(sp, srcI, src, idx_in)
            sp.dma_start(srcI[FULL:P, REST:TL], src[0:TL - REST].rearrange("(a t) -> a t", a=1)).then_inc(idx_in, 16)
            load_cols(sp, typI, typ, idx_in)
            sp.dma_start(typI[FULL:P, REST:TL], typ[0:TL - REST].rearrange("(a t) -> a t", a=1)).then_inc(idx_in, 16)
            sp.wait_ge(fills, 4)
            load_cols(sp, dstI, dst, idx_in)
            sp.dma_start(prevI[0:1, 1:TL], dst[0:TL - 1].rearrange("(a t) -> a t", a=1)).then_inc(idx_in, 16)
            sp.dma_start(prevI[1:FULL, :], dst[TL - 1:FULL * TL - 1].rearrange("(p t) -> p t", t=TL)).then_inc(idx_in, 16)
            sp.dma_start(prevI[FULL:P, 0:REST], dst[FULL * TL - 1:E - 1].rearrange("(a t) -> a t", a=1)).then_inc(idx_in, 16)
            sp.dma_start(nextI[0:FULL, :], dst[1:FULL * TL + 1].rearrange("(p t) -> p t", t=TL)).then_inc(idx_in, 16)
            sp.dma_start(nextI[FULL:P, 0:REST - 1], dst[FULL * TL + 1:E].rearrange("(a t) -> a t", a=1)).then_inc(idx_in, 16)
            sp.dma_start(aboveI[1:P, :], dst[0:FULL * TL].rearrange("(p t) -> p t", t=TL)).then_inc(idx_in, 16)
            sp.dma_start(w_sm[:, 0, :], w_msg).then_inc(par_in, 16)
            sp.dma_start(w_sm[:, 1, :], w_node).then_inc(par_in, 16)
            sp.dma_start(w_sm[:, 2, :], w_edge).then_inc(par_in, 16)
            sp.dma_start(bcol[:, 0:1], b_node.unsqueeze(1)).then_inc(par_in, 16)
            sp.dma_start(bcol[:, 1:2], b_edge.unsqueeze(1)).then_inc(par_in, 16)
            sp.dma_start(bm_row, b_msg.unsqueeze(0).to_broadcast([P, D])).then_inc(par_in, 16)
            sp.dma_start(bias_row[:, 0, :], bias[0:1, :].to_broadcast([P, D])).then_inc(par_in, 16)
            sp.dma_start(bias_row[:, 1, :], bias[1:2, :].to_broadcast([P, D])).then_inc(par_in, 16)
            for j in range(2):
                sp.dma_start(qk[:, j, 0:1], att_q[j]).then_inc(par_in, 16)
                sp.dma_start(qk[:, j, 1:2], att_k[j]).then_inc(par_in, 16)
            sp.dma_start(w_all, w_rel.rearrange("l r f g -> f (l r) g")).then_inc(par_in, 16)
            sp.dma_start(wr[:], w_rel[0].rearrange("r f g -> f r g")).then_inc(w0_in, 16)
            sp.dma_start(ys[0:FULL, :, :], ea[0:FULL * TL].rearrange("(p t) d -> p t d", t=TL)).then_inc(ea_in, 16)
            sp.dma_start(ys[FULL:P, 0:REST, :], ea[FULL * TL:E].unsqueeze(0)).then_inc(ea_in, 16)
            sp.dma_start(ys[FULL:P, REST:TL, :], ea[0:TL - REST].unsqueeze(0)).then_inc(ea_in, 16)
            for c in range(SLOTS):
                sp.dma_start(slot(c), x_bulk[:, c * BR:(c + 1) * BR, :]).then_inc(bulk_in[c], 16)
            sp.wait_ge(idx_Tsb, 2)
            sp.dma_start(src_cols, colsT[0:TL, 0:P]).then_inc(cols_out, 16)
            sp.dma_start(typ_cols, typT8[0:TL, :]).then_inc(cols_out, 16)
            sp.wait_ge(cols_out, 32)
            sp.dma_start(typB[:].rearrange("p t q -> p (t q)"),
                         typ_cols.rearrange("t q -> (t q)").unsqueeze(0).to_broadcast([P, EP])).then_inc(typB_in, 16)
            src_flat = src_cols.rearrange("t q -> (t q)").unsqueeze(0)
            for u in range(2):
                sp.dma_start(work[:, u, :], src_flat[:, u * G * P:(u + 1) * G * P].to_broadcast([P, G * P])).then_inc(srcB_in[u], 16)

            def bulk_step(k, b):
                sp.wait_ge(b_norm2, k)
                sp.dma_start(o_bulk[:, bass.ds((k - 1) * BR, BR), :] if not isinstance(k, int) else
                             o_bulk[:, (k - 1) * BR:k * BR, :], slot(b)).then_inc(bulk_out[b], 16)
                if isinstance(k, int) and k + SLOTS - 1 > BC:
                    return
                sp.wait_ge(bulk_out[b], (k - 1 - b) * (16 // SLOTS) + 16)
                if isinstance(k, int) and k + SLOTS - 1 == BC:
                    sp.dma_start(slot(b)[0:BREM, 0, :], x[BC * BR * P:N]).then_inc(bulk_in[b], 16)
                    return
                c = k + SLOTS - 1
                sp.dma_start(slot(b), x_bulk[:, bass.ds(c * BR, BR), :] if not isinstance(k, int) else
                             x_bulk[:, c * BR:(c + 1) * BR, :]).then_inc(bulk_in[b], 16)

            with sp.Fori(0, NG) as i:
                for u in range(SLOTS):
                    bulk_step(i * SLOTS + (u + 1), u)
            for k in range(NG * SLOTS + 1, BC + 1):
                bulk_step(k, (k - 1) % SLOTS)
            sp.wait_ge(b_norm2, BC + 1)
            sp.dma_start(out[BC * BR * P:N], slot(BC)[0:BREM, 0, :]).then_inc(bulk_out[BC % SLOTS], 16)

            with sp.Fori(0, NG // 2 - 1) as i:
                for u in range(2):
                    sp.wait_ge(p_step, i * 2 + (u + 1))
                    sp.dma_start(work[:, u, :], src_flat[:, bass.ds((i * 2 + (u + 2)) * (G * P), G * P)]
                                 .to_broadcast([P, G * P])).then_inc(srcB_in[u], 16)

            for j in range(2):
                rows, buf = tables[j][1], (xd, ys)[j]
                if j == 1:
                    sp.wait_ge(m_used[0], NG * R + 2)
                    sp.dma_start(wr[:], w_rel[1].rearrange("r f g -> f r g")).then_inc(w1_in, 16)
                with sp.Fori(0, NG // 2) as i:
                    for u in range(2):
                        sp.wait_ge(f_rows[j], i * 2 + (u + 1))
                        sp.dma_start(grp(rows, i * 2 + u), grp(buf, i * 2 + u)).then_inc(tab_out[j][u], 16)

        @block.gpsimd
        def _(pool):
            nc.gpsimd.memset(prevI, -1).then_inc(fills, 1)
            nc.gpsimd.memset(nextI, -1).then_inc(fills, 1)
            nc.gpsimd.memset(aboveI, -1).then_inc(fills, 1)
            nc.gpsimd.memset(dstI[:], N).then_inc(fills, 1)
            nc.gpsimd.memset(ones[:], 1.0).then_inc(consts, 1)
            nc.gpsimd.memset(epsc[:], EPS).then_inc(consts, 1)
            nc.gpsimd.memset(identS[:], 0.0).then_inc(consts, 1)
            nc.gpsimd.memset(sel0[:], 0.0).then_inc(consts, 1)
            nc.gpsimd.memset(turn[:], 0.0).then_inc(consts, 1)
            pool.wait_ge(consts, 5)
            nc.gpsimd.affine_select(out=identS[:], in_=identS[:], compare_op=ALU.not_equal, fill=1.0, base=1,
                                    pattern=[[-1, P + 2]], channel_multiplier=1).then_inc(consts, 1)
            nc.gpsimd.affine_select(out=sel0[:], in_=sel0[:], compare_op=ALU.not_equal, fill=1.0, base=0,
                                    pattern=[[0, P]], channel_multiplier=1).then_inc(consts, 1)

            def gather(buf, table, idx, sems, bound, ready=None):
                for g in range(NG):
                    u = g % 2
                    if g >= 2:
                        pool.wait_ge(sems[u], 16 * G * (g // 2))
                    if ready:
                        pool.wait_ge(ready, g + 1)
                    for t in range(g * G, g * G + G):
                        extra = {} if bound is None else dict(bounds_check=bound, oob_is_err=False)
                        nc.gpsimd.indirect_dma_start(
                            out=buf[:, t, :], out_offset=None, in_=table,
                            in_offset=bass.IndirectOffsetOnAxis(ap=idx[:, t:t + 1], axis=0), **extra).then_inc(sems[u], 16)

            pool.wait_ge(idx_in, 16 * N_IDX)
            gather(xs, x, srcI, xs_in[0], None)
            pool.wait_ge(prol_d, 1)
            pool.wait_ge(cols_out, 32)
            pool.wait_ge(mix_s, 2)
            pool.wait_ge(wqk_p, 1)
            gather(xd, x, dstG, xd_in, None)
            for j in range(2):
                pool.wait_ge(p_ready, 1)
                for u in range(2):
                    pool.wait_ge(tab_out[j][u], 16 * NG // 2)
                if j == 1:
                    pool.wait_ge(m_T[0], NG)
                    for g in range(NG):
                        nc.gpsimd.tensor_copy(grp(xs, g), mid(relu_row[:, 0, :], G)).then_inc(refill, 1)
                gather(xs, tables[j][0], posI, xs_in[j + 1], EP - 1, ready=(a_norm, refill)[j])
            for b in range(SLOTS):
                pool.wait_ge(bulk_out[b], 16 * len(range(b, BC + 1, SLOTS)))
            for g in range(NG):
                pool.wait_ge(f_rows[2], g + 1)
                for t in range(g * G, g * G + G):
                    nc.gpsimd.indirect_dma_start(
                        out=out, out_offset=bass.IndirectOffsetOnAxis(ap=outI[:, t:t + 1], axis=0),
                        in_=xd[:, t, :], in_offset=None, bounds_check=N - 1, oob_is_err=False).then_inc(rows_out, 16)
            pool.wait_ge(rows_out, 16 * TL)

        @block.tensor
        def _(pe):
            pe.wait_ge(consts, 7)
            pe.wait_ge(idx_f, 1)
            pe.transpose(ps_s[0:TL, 0:P], srcF, ident)
            pe.transpose(ps_s[0:TL, P:2 * P], typF[:], ident).then_inc(idx_T, 1)
            pe.wait_ge(par_in, 16 * N_PAR)
            pe.transpose(ps_t[:, 0:P], w_sm[:, 0, :], ident).then_inc(wmT_p, 1)
            for a in range(2 * R):
                mm = pe.transpose(ps_y[:, a // R, a % R * P:(a % R + 1) * P], w_all[:, a, :], ident)
            mm.then_inc(wrT_p, 1)
            pe.wait_ge(diag_r, 1)
            pe.wait_ge(idx_Tsb, 2)
            pe.matmul(ps_s[:, 2 * P:4 * P], ones[:], diags, start=True, stop=True).then_inc(diag_p, 1)
            pe.wait_ge(wmT_s, 1)
            pe.matmul(ps_t[:, P:2 * P], w_sm[:, 1, :], w_mT, start=True, stop=True)
            pe.matmul(ps_t[:, 2 * P:3 * P], w_sm[:, 2, :], w_mT, start=True, stop=True)
            pe.wait_ge(brep_r, 1)
            pe.matmul(ps_t[:, 3 * P:4 * P], b_rep, w_mT, start=True, stop=True).then_inc(mix_p, 1)
            pe.wait_ge(wrT_s, 1)
            for a in range(2 * R):
                mm = pe.matmul(ps_k[:, 2 * a:2 * a + 2], wT[:, a, :], qk[:, a // R, :], start=True, stop=True)
            mm.then_inc(wqk_p, 1)

            pe.wait_ge(mix_s, 2)
            pe.wait_ge(c_r, 1)
            pe.wait_ge(ea_in, 48)
            for g in range(NG):
                u = g % 2
                pe.wait_ge(xs_in[0][u], (g // 2 + 1) * (16 * G))
                pe.wait_ge(a_Ts, g * 2 + 1)
                for t in range(G):
                    mm = pe.transpose(ps_t[:, t * P:(t + 1) * P], row_of(xs, g * G + t), ident)
                mm.then_inc(a_T, 1)
                pe.wait_ge(a_Ts, g * 2 + 2)
                for t in range(G):
                    mm = pe.transpose(ps_t[:, t * P:(t + 1) * P], row_of(ys, g * G + t), ident)
                mm.then_inc(a_T, 1)
                pe.wait_ge(a_Ts, g * 2 + 3)
                pe.wait_ge(a_ys, g + 1)
                for t in range(G):
                    o = ps_y[:, u, t * P:(t + 1) * P]
                    pe.matmul(o, opT[:, 0, t * P:(t + 1) * P], m_node[:], start=True, stop=False)
                    pe.matmul(o, opT[:, 1, t * P:(t + 1) * P], m_edge[:], start=False, stop=False)
                    mm = pe.matmul(o, sel0[:], c_row[:], start=False, stop=True)
                mm.then_inc(a_msg, 1)

            with pe.Fori(0, NG // 2) as i:
                for u in range(2):
                    g = i * 2 + u
                    pe.wait_ge(p_step, g + 1)
                    for t in range(G):
                        o = ps_y[:, u, t * P:t * P + TL + 1]
                        st_t = stepT[:, u, t * P:(t + 1) * P]
                        pe.matmul(o, st_t, colbf[:, 0, :], start=True, stop=False)
                        mm = pe.matmul(o, st_t, colbf[:, 1, :], start=False, stop=True)
                    mm.then_inc(p_row, 1)

            uses = [0]

            def carry_product(mat, rhs, n):
                uses[0] += 1
                pe.wait_ge(cy_in, uses[0])
                pe.matmul(ps_s[:, 0:n], mat, rhs, start=True, stop=True).then_inc(cy_ps, 1)

            def carry_turn():
                uses[0] += 1
                pe.wait_ge(cy_in, uses[0])
                pe.transpose(ps_s[:, 0:P], turn[:, 0:P], ident).then_inc(cy_ps, 1)

            def node_scores(j):
                buf = (xd, ys)[j]
                for g in range(NG):
                    u = g % 2
                    pe.wait_ge(f_rows[j], g + 1)
                    pe.wait_ge(f_Ts[j], g + 1)
                    for t in range(G):
                        mm = pe.transpose(ps_t[:, t * P:(t + 1) * P], row_of(buf, g * G + t), ident)
                    mm.then_inc(f_T[j], 1)
                    pe.wait_ge(f_Ts[j], g + 2)
                    pe.wait_ge(f_qs[j], g + 1)
                    for t in range(G):
                        mm = pe.matmul(ps_k[:, t * R:(t + 1) * R], opT[:, u, t * P:(t + 1) * P], wqk[:, j, :, 0],
                                       start=True, stop=True)
                    mm.then_inc(f_q[j], 1)

            def relation_products(j):
                pe.wait_ge((w0_in, w1_in)[j], 16)

                def turn_rows(g, u, rows_in):
                    pe.wait_ge(xs_in[j + 1][u], rows_in)
                    pe.wait_ge(m_Ts[j], g + 1)
                    for t in range(G):
                        mm = pe.transpose(ps_t[:, t * P:(t + 1) * P], row_of(xs, g * G + t), ident)
                    mm.then_inc(m_T[j], 1)

                def key_scores(g, u):
                    pe.wait_ge(m_Ts[j], g + 2)
                    pe.wait_ge(m_ks[j], g + 1)
                    for t in range(G):
                        mm = pe.matmul(ps_k[:, t * R:(t + 1) * R], opT[:, u, t * P:(t + 1) * P],
                                       wqk[:, j, :, 1], start=True, stop=True)
                    mm.then_inc(m_k[j], 1)

                def products(g, u):
                    pe.wait_ge(m_ys[j], g + 1)
                    for r in range(R):
                        pe.wait_ge(m_mask[j], g * R + (r + 1 + 2 * R))
                        for t in range(G):
                            mm = pe.matmul(ps_y[:, u, t * P:(t + 1) * P], work[:, r % 2, t * P:(t + 1) * P],
                                           wr[:, r, :], start=(r == 0 and t % 4 == 0), stop=(r == R - 1),
                                           skip_group_check=True)
                        mm.then_inc(m_used[j], 1)

                pe.sem_inc(m_used[j], 2)
                turn_rows(0, 0, 16 * G)
                key_scores(0, 0)
                for g in range(NG):
                    u = g % 2
                    if g < NG - 1:
                        turn_rows(g + 1, 1 - u, ((g + 1) // 2 + 1) * (16 * G))
                    products(g, u)
                    if g < NG - 1:
                        key_scores(g + 1, 1 - u)

            carry_product(carryF[:], t0[:, TL - 1:TL], 1)
            carry_product(carryF[:], ys[:, TL - 1, :], P)
            node_scores(0)
            for j in range(2):
                carry_product(carryB[:], q8[:, 0, :], R)
                relation_products(j)
                carry_turn()
                carry_turn()
                carry_product(carryB[:], mx[:, 0:1], 1)
                carry_product(carryF[:], fm[:, TL - 1:TL], 1)
                carry_product(carryF[:], ys[:, TL - 1, :], P)
                if j == 0:
                    node_scores(1)

        @block.scalar
        def _(act):
            a = nc.scalar

            def copy(o, i_):
                return a.activation(o, i_, ACT.Copy)

            act.sem_inc(a_Ts, 1)
            act.sem_inc(a_ys, 2)
            for j in range(2):
                act.sem_inc(m_ks[j], 1)
                act.sem_inc(f_qs[j], 1)
                act.sem_inc(f_Ts[j], 1)
                act.sem_inc(m_Ts[j], 1)
                act.sem_inc(m_ys[j], 2)
            act.wait_ge(idx_T, 1)
            copy(colsT[0:TL, 0:P], ps_s[0:TL, 0:P]).then_inc(idx_Tsb, 1)
            copy(typT8[0:TL, :], ps_s[0:TL, P:2 * P]).then_inc(idx_Tsb, 1)
            act.wait_ge(wmT_p, 1)
            copy(w_mT, ps_t[:, 0:P]).then_inc(wmT_s, 1)
            act.wait_ge(wrT_p, 1)
            copy(wT[:, 0:R, :], ps_y[:, 0, :].rearrange("p (a b) -> p a b", b=P))
            copy(wT[:, R:2 * R, :], ps_y[:, 1, :].rearrange("p (a b) -> p a b", b=P)).then_inc(wrT_s, 1)
            act.wait_ge(mix_p, 1)
            copy(m_node[:], ps_t[:, P:2 * P]).then_inc(mix_s, 1)
            copy(m_edge[:], ps_t[:, 2 * P:3 * P]).then_inc(mix_s, 1)
            act.wait_ge(wqk_p, 1)
            copy(wqk[:].rearrange("p l r a -> p (l r a)"), ps_k[:, 0:4 * R]).then_inc(wqk_s, 1)

            def bulk_step(k, kb, first=True, second=True):
                h, lo, hi = kb % 2, 0 if first else BR, 2 * BR if second else BR
                act.wait_ge(b_sum, k + 1)
                a.activation(sd[:, h, lo:hi], df[:, h, lo:hi], ACT.Sqrt, bias=epsc[:, 0:1], scale=1.0 / D).then_inc(b_sd, 1)
                act.wait_ge(b_rs, k + 1)
                for half, c, s_ in ((0, kb, b_norm1), (1, kb - 1, b_norm2)):
                    if not (first, second)[half]:
                        continue
                    for r in range(BR):
                        n = half * BR + r
                        ins = a.activation(slot(c)[:, r, :], slot(c)[:, r, :], ACT.Identity,
                                           bias=nm[:, h, n:n + 1], scale=rs[:, h, n:n + 1])
                    ins.then_inc(s_, 1)

            def out_of_psum(o, i_, producer, n, done):
                act.wait_ge(producer, n)
                copy(o, i_).then_inc(done, 1)

            bulk_step(0, 0, second=False)
            with act.Fori(0, NG // 2) as i:
                for u in range(2):
                    g = i * 2 + u
                    k = i * (2 * SLOTS) + (SLOTS * u + 1)
                    bulk_step(k, 1)
                    out_of_psum(opT[:, 0, :], ps_t[:, 0:GD], a_T, g * 2 + 1, a_Ts)
                    bulk_step(k + 1, 2)
                    out_of_psum(opT[:, 1, :], ps_t[:, 0:GD], a_T, g * 2 + 2, a_Ts)
                    bulk_step(k + 2, 3)
                    out_of_psum(grp(ys, g).rearrange("p a b -> p (a b)"), ps_y[:, u, 0:GD], a_msg, g + 1, a_ys)
                    bulk_step(k + 3, 0)
                    act.wait_ge(a_sum, g + 1)
                    a.activation(sd7[:], df7[:], ACT.Sqrt, bias=epsc[:, 0:1], scale=1.0 / D).then_inc(a_sd, 1)
                    act.wait_ge(a_rs, g + 1)
                    for t in range(G):
                        ins = a.activation(row_of(xs, g * G + t), row_of(xs, g * G + t), ACT.Identity,
                                           bias=nm7[:, u, t:t + 1], scale=rs7[:, u, t:t + 1])
                    ins.then_inc(a_norm, 1)
            for k in range(NG * SLOTS + 1, BC + 2):
                bulk_step(k, k % SLOTS, first=k <= BC)

            def norm_rows(j, g, u):
                act.wait_ge(f_sum[j], g + 1)
                a.activation(sd7[:], df7[:], ACT.Sqrt, bias=epsc[:, 0:1], scale=1.0 / D).then_inc(f_sd[j], 1)
                act.wait_ge(f_rs[j], g + 1)
                for t in range(G):
                    ins = a.activation(row_of(xd, g * G + t), row_of(xd, g * G + t), ACT.Identity,
                                       bias=nm7[:, u, t:t + 1], scale=rs7[:, u, t:t + 1])
                ins.then_inc(f_rows[j], 1)

            def query_scores_out(j, g, u):
                out_of_psum(opT[:, u, :], ps_t[:, 0:GD], f_T[j], g + 1, f_Ts[j])
                out_of_psum(grp(q8, g), ps_k[:, 0:G * R].rearrange("p (t r) -> p t r", r=R),
                            f_q[j], g + 1, f_qs[j])

            with act.Fori(0, NG // 2) as i:
                for u in range(2):
                    norm_rows(0, i * 2 + u, u)
                    query_scores_out(0, i * 2 + u, u)

            for j in range(2):
                def rows_T(g, u):
                    act.wait_ge(m_mask[j], (g + 1) * R)
                    out_of_psum(opT[:, u, :], ps_t[:, 0:GD], m_T[j], g + 1, m_Ts[j])

                def products_out(g, u):
                    out_of_psum(grp(ys, g).rearrange("p a b -> p (a b)"), ps_y[:, u, 0:GD],
                                m_used[j], (g + 1) * R + 2, m_ys[j])

                def key_scores_out(g, u):
                    out_of_psum(grp(k8, g), ps_k[:, 0:G * R].rearrange("p (t r) -> p t r", r=R),
                                m_k[j], g + 1, m_ks[j])

                rows_T(0, 0)
                key_scores_out(0, 0)
                with act.Fori(0, NG // 2 - 1) as i:
                    for u in range(2):
                        rows_T(i * 2 + (u + 1), 1 - u)
                        products_out(i * 2 + u, u)
                        key_scores_out(i * 2 + (u + 1), 1 - u)
                rows_T(NG - 1, 1)
                products_out(NG - 2, 0)
                key_scores_out(NG - 1, 1)
                products_out(NG - 1, 1)
                act.wait_ge(s_arg[j], 1)
                a.activation(lg[:], lg[:], ACT.Exp).then_inc(s_exp[j], 1)
                act.wait_ge(s_exp[j], 1)
                act.wait_ge(m_ys[j], NG + 2)
                with act.Fori(0, NG) as g:
                    for t in range(G):
                        ins = a.activation(row_of(ys, g * G + t), row_of(ys, g * G + t), ACT.Copy, scale=at(lg, g * G + t))
                    ins.then_inc(n_y[j], 1)
                if j == 0:
                    with act.Fori(0, NG // 2) as i:
                        for u in range(2):
                            g = i * 2 + u
                            act.wait_ge(f_sum[1], g + 1)
                            a.activation(grp(ys, g), grp(ys, g), ACT.Relu).then_inc(f_rows[1], 1)
                            query_scores_out(1, g, u)
                else:
                    with act.Fori(0, NG // 2) as i:
                        for u in range(2):
                            norm_rows(2, i * 2 + u, u)

        @block.vector
        def _(dve):
            v = nc.vector
            T = Tally(dve, pro)
            STT, TT, TS = v.scalar_tensor_tensor, v.tensor_tensor, v.tensor_scalar

            for j in range(2):
                dve.sem_inc(m_mask[j], 2 * R)
            dve.wait_ge(idx_in, 16 * N_IDX)
            T.of(v.tensor_copy(srcF, srcI[:]))
            T.of(v.tensor_copy(typF[:], typI))
            T.of(v.tensor_copy(dstF, dstI[:]))
            T.of(v.tensor_copy(first[:], dstI[:, 0:1]))
            T.of(TT(same[:], dstI[:], prevI, ALU.is_equal))
            T.of(TT(nxt[:], dstI[:], nextI, ALU.is_equal))
            T.of(TS(dstG[:], dstI[:], float(N - 1), None, ALU.min))
            T.step(TT(diffI, dstI[:], aboveI, ALU.subtract))
            T.step(TS(src1[:], srcF, 1.0, None, ALU.add))
            dve.sem_inc(idx_f, 1)
            T.of(v.tensor_tensor_scan(pre[:], same[:], same[:], 1.0, ALU.mult, ALU.min))
            T.of(v.tensor_tensor_scan(suf[:, ::-1], nxt[:, ::-1], nxt[:, ::-1], 1.0, ALU.mult, ALU.min))
            T.of(STT(t0[:], nxt[:], SKIP, dstF, ALU.mult, ALU.add))
            T.of(TS(lowI, diffI, 255, None, ALU.bitwise_and))
            T.step(v.memset(colbf[:, 0, TL:TL + 1], 1.0))
            T.of(v.memset(colbf[:, 1, TL:TL + 1], 0.0))
            T.of(v.tensor_copy(outI[:], t0[:]))
            T.of(TT(colbf[:, 0, 0:TL], diffI, lowI, ALU.subtract))
            T.of(v.tensor_copy(colbf[:, 1, 0:TL], lowI))
            dve.wait_ge(consts, 7)
            T.of(TS(diags[:, 0:P], ident, pre[:, TL - 1:TL], None, ALU.mult))
            T.step(TS(diags[:, P:2 * P], ident, suf[:, 0:1], None, ALU.mult))
            dve.sem_inc(diag_r, 1)
            dve.wait_ge(par_in, 16 * N_PAR)
            T.step(TT(bcol[:, 2:3], bcol[:, 0:1], bcol[:, 1:2], ALU.add))
            T.of(TS(relu_row[:], bias_row[:], 0.0, None, ALU.max))
            T.step(TS(b_rep, ones[:], bcol[:, 2:3], None, ALU.mult))
            dve.sem_inc(brep_r, 1)
            dve.wait_ge(diag_p, 1)
            T.of(v.memset(spread[:, 0:1], 0.0))
            T.of(v.memset(spread[:, 2 * P + 1:2 * P + 2], 0.0))
            T.of(v.tensor_copy(spread[:, 1:2 * P + 1], ps_s[:, 2 * P:4 * P]))
            T.step(TS(far[0:1, :], ps_s[0:1, 2 * P:3 * P], 1.0, BIG, ALU.subtract, ALU.mult))
            T.of(v.tensor_tensor_scan(carryF[:], spread[:, 0:P], identS[:, 0:P], 0.0, ALU.mult, ALU.add))
            T.step(v.tensor_tensor_scan(carryB[:, ::-1], spread[:, P + 2:2 * P + 2][:, ::-1], identS[:, 2:P + 2][:, ::-1],
                                        0.0, ALU.mult, ALU.add))
            dve.wait_ge(mix_s, 2)
            T.step(TT(c_row[:], ps_t[:, 3 * P:4 * P], bm_row, ALU.add))
            dve.sem_inc(c_r, 1)
            dve.sem_inc(prol_d, 1)

            def sums(stats, s2, d):
                T.of(TT(s2, stats[:, :, 1:3], stats[:, :, 4:6], ALU.add))
                T.step(TT(d, stats[:, :, 1], stats[:, :, 4], ALU.subtract))
                T.step(STT(d, d, 32.0, d, ALU.mult, ALU.mult))
                return TT(d, d, s2[:, :, 1], ALU.add)

            def scales(dev, s2, r_, n_):
                T.step(v.reciprocal(r_, dev))
                return STT(n_, s2[:, :, 0], -0.5, r_, ALU.mult, ALU.mult)

            def bulk_step(k, kb, first=True, second=True):
                h, lo, hi = kb % 2, 0 if first else BR, 2 * BR if second else BR
                if first:
                    dve.wait_ge(bulk_in[kb], (k - kb) * (16 // SLOTS) + 16)
                    for r in range(BR):
                        ins = T.of(v.bn_stats(st[:, h, r, :], slot(kb)[:, r, :]))
                if second:
                    dve.wait_ge(b_norm1, k)
                    T.step(TT(slot(kb - 1), slot(kb - 1), mid(relu_row[:, 1, :], BR), ALU.add))
                    for r in range(BR):
                        ins = T.of(v.bn_stats(st[:, h, BR + r, :], slot(kb - 1)[:, r, :]))
                T.wait()
                sums(st[:, h, lo:hi, :], sm[:, h, lo:hi, :], df[:, h, lo:hi]).then_inc(b_sum, 1)
                dve.wait_ge(b_sd, k + 1)
                scales(sd[:, h, lo:hi], sm[:, h, lo:hi, :], rs[:, h, lo:hi], nm[:, h, lo:hi]).then_inc(b_rs, 1)

            def scan_rows(g):
                for t in range(G):
                    c = g * G + t
                    T.step(STT(row_of(ys, c), row_of(ysz, c), at(same, c), row_of(ys, c), ALU.mult, ALU.add))

            def stats7(buf, g):
                T.of(v.memset(tick[:], 0.0))
                for t in range(G):
                    T.of(v.bn_stats(st7[:, t, :], row_of(buf, g * G + t)))
                T.wait()

            T.step(v.memset(ysz[:, 0, :], 0.0))
            bulk_step(0, 0, second=False)
            with dve.Fori(0, NG // 2) as i:
                T.enter(i, LOOP_A)
                for u in range(2):
                    g = i * 2 + u
                    for q in range(SLOTS):
                        bulk_step(i * (2 * SLOTS) + (SLOTS * u + q + 1), (q + 1) % SLOTS)
                    dve.wait_ge(xs_in[0][u], i * (16 * G) + 16 * G)
                    stats7(xs, g)
                    sums(st7[:], sm7[:], df7[:]).then_inc(a_sum, 1)
                    dve.wait_ge(a_ys, g + 3)
                    scan_rows(g)
                    dve.wait_ge(a_sd, g + 1)
                    scales(sd7[:], sm7[:], rs7[:, u, :], nm7[:, u, :]).then_inc(a_rs, 1)
            T.leave(NG // 2)
            for k in range(NG * SLOTS + 1, BC + 2):
                bulk_step(k, k % SLOTS, first=k <= BC)

            def steps(g, u, arrived):
                dve.wait_ge(srcB_in[u], arrived)
                TS(stepT[:, u, 0:GD], work[:, u, :], first[:, 0:1], None, ALU.is_ge).then_inc(p_step, 1)

            def search(g, u):
                dve.wait_ge(p_row, g + 1)
                rows = ps_y[:, u, :].rearrange("p (t c) -> p t c", c=P)[:, 0:G, :]
                mine = wide(grpc(src1, g), TL)
                T.step(TT(posw, rows[:, :, 0:TL], mine, ALU.is_le))
                T.of(v.tensor_reduce(grpc(posn, g), posw, AX.X, ALU.add))
                T.step(TS(grpc(post, g), rows[:, :, TL], float(TL), None, ALU.mult))
                T.step(TT(posw, rows[:, :, 0:TL], mine, ALU.is_equal))
                T.step(v.tensor_reduce(grpc(lg, g), posw, AX.X, ALU.max))

            for b in range(SLOTS):
                dve.wait_ge(bulk_out[b], 16 * len(range(b, BC + 1, SLOTS)))
            dve.wait_ge(a_msg, NG)
            steps(0, 0, 16)
            steps(1, 1, 16)
            with dve.Fori(0, NG // 2 - 1) as i:
                T.enter(i, LOOP_P)
                for u in range(2):
                    search(i * 2 + u, u)
                    steps(i * 2 + (u + 2), u, i * 16 + 32)
            T.leave(NG // 2 - 1)
            search(NG - 2, 0)
            search(NG - 1, 1)
            T.step(TT(posn, posn, post, ALU.add))
            T.step(TS(lg[:], lg[:], -SKIP, SKIP - TL - 1.0, ALU.mult, ALU.add))
            T.step(TT(lg[:], lg[:], posn, ALU.add))
            T.step(v.tensor_copy(posI[:], lg[:]))
            dve.sem_inc(p_ready, 1)

            uses = [0]

            def carried():
                uses[0] += 1
                dve.sem_inc(cy_in, 1)
                dve.wait_ge(cy_ps, uses[0])

            def carried_rows():
                carried()
                T.step(v.tensor_copy(carry[:], ps_s[:, 0:P]))

            T.step(v.tensor_tensor_scan(t0[:], same[:], ones[:, 0:TL], 0.0, ALU.mult, ALU.add))
            carried()
            T.step(STT(t0[:], pre[:], ps_s[:, 0:1], t0[:], ALU.mult, ALU.add))
            T.step(v.reciprocal(rcp[:], t0[:]))
            carried_rows()

            def whole_sums(g):
                for t in range(G):
                    c = g * G + t
                    T.of(STT(row_of(ys, c), carry[:], at(pre, c), row_of(ys, c), ALU.mult, ALU.add))
                T.wait()

            with dve.Fori(0, NG // 2) as i:
                T.enter(i, LOOP_F0)
                for u in range(2):
                    g = i * 2 + u
                    whole_sums(g)
                    dve.wait_ge(xd_in[u], i * (16 * G) + 16 * G)
                    for t in range(G):
                        c = g * G + t
                        T.of(STT(row_of(xd, c), row_of(ys, c), at(rcp, c), row_of(xd, c), ALU.mult, ALU.add))
                    T.wait()
                    stats7(xd, g)
                    sums(st7[:], sm7[:], df7[:]).then_inc(f_sum[0], 1)
                    dve.wait_ge(f_sd[0], g + 1)
                    scales(sd7[:], sm7[:], rs7[:, u, :], nm7[:, u, :]).then_inc(f_rs[0], 1)
            T.leave(NG // 2)
            for r in range(R):
                T.of(TS(hot[:, :, r], typF[:], float(r), None, ALU.is_equal))

            for j in range(2):
                dve.wait_ge(f_qs[j], NG + 1)
                T.step(TT(tmp8, q8, wide(nxt[:], R), ALU.mult))
                T.step(TT(q8, q8, tmp8, ALU.subtract))
                for r in range(R):
                    T.of(v.tensor_tensor_scan(q8[:, ::-1, r], nxt[:, ::-1], q8[:, ::-1, r], 0.0, ALU.mult, ALU.add))
                T.wait()
                carried()
                for r in range(R):
                    T.of(STT(q8[:, :, r], suf[:], ps_s[:, r:r + 1], q8[:, :, r], ALU.mult, ALU.add))
                T.wait()
                if j == 0:
                    dve.wait_ge(typB_in, 16)
                with dve.Fori(0, NG // 2) as i:
                    for u in range(2):
                        g = i * 2 + u
                        dve.wait_ge(m_Ts[j], g + 2)
                        for r in range(R):
                            dve.wait_ge(m_used[j], g * R + (r + 1))
                            STT(work[:, r % 2, :], grp(typB, g).rearrange("p a b -> p (a b)"), float(r),
                                opT[:, u, :], ALU.is_equal, ALU.mult).then_inc(m_mask[j], 1)
                dve.wait_ge(m_ks[j], NG + 1)
                T.step(TT(tmp8, k8, q8, ALU.add))
                T.step(TT(tmp8, tmp8, hot, ALU.mult))
                T.step(v.tensor_reduce(t0[:], tmp8, AX.X, ALU.add))
                T.step(STT(lg[:], t0[:], SLOPE, t0[:], ALU.mult, ALU.max))
                T.step(TS(t0[:], same[:], 1.0, BIG, ALU.subtract, ALU.mult))
                T.step(v.tensor_tensor_scan(fm[:], t0[:], lg[:], -BIG, ALU.add, ALU.max))
                T.step(v.tensor_copy(turn[:, 0:1], fm[:, TL - 1:TL]))
                carried()
                T.of(v.tensor_tensor_scan(turn[0:1, 1:P + 1], far[0:1, :], ps_s[0:1, 0:P], -BIG, ALU.add, ALU.max))
                T.step(v.memset(turn[0:1, 0:1], -BIG))
                carried()
                T.step(v.tensor_copy(mx[:, 0:1], ps_s[:, 0:1]))
                T.step(v.tensor_tensor_scan(fm[:], t0[:], lg[:], mx[:, 0:1], ALU.add, ALU.max))
                T.step(TT(t0[:], nxt[:], fm[:], ALU.mult))
                T.step(TT(t0[:], fm[:], t0[:], ALU.subtract))
                T.step(v.tensor_tensor_scan(mx[:, ::-1], nxt[:, ::-1], t0[:, ::-1], 0.0, ALU.mult, ALU.add))
                carried()
                T.step(STT(mx[:], suf[:], ps_s[:, 0:1], mx[:], ALU.mult, ALU.add))
                T.step(TT(lg[:], lg[:], mx[:], ALU.subtract))
                dve.sem_inc(s_arg[j], 1)
                dve.wait_ge(s_exp[j], 1)
                T.step(v.tensor_tensor_scan(fm[:], same[:], lg[:], 0.0, ALU.mult, ALU.add))
                carried()
                T.step(STT(fm[:], pre[:], ps_s[:, 0:1], fm[:], ALU.mult, ALU.add))
                T.step(TS(fm[:], fm[:], 1e-16, None, ALU.add))
                T.step(v.reciprocal(rcp[:], fm[:]))
                with dve.Fori(0, NG) as g:
                    T.enter(g, G)
                    dve.wait_ge(n_y[j], g + 1)
                    scan_rows(g)
                T.leave(NG)
                carried_rows()
                with dve.Fori(0, NG // 2) as i:
                    T.enter(i, LOOP_F[j])
                    for u in range(2):
                        g = i * 2 + u
                        whole_sums(g)
                        for t in range(G):
                            c = g * G + t
                            ins = STT(row_of(ys, c), row_of(ys, c), at(rcp, c), bias_row[:, j, :], ALU.mult, ALU.add)
                            if j == 1 or t < G - 1:
                                T.of(ins)
                        if j == 0:
                            ins.then_inc(f_sum[1], 1)
                            continue
                        T.wait()
                        T.step(STT(grp(xd, g), grp(ys, g), 0.0, grp(xd, g), ALU.max, ALU.add))
                        stats7(xd, g)
                        sums(st7[:], sm7[:], df7[:]).then_inc(f_sum[2], 1)
                        dve.wait_ge(f_sd[2], g + 1)
                        scales(sd7[:], sm7[:], rs7[:, u, :], nm7[:, u, :]).then_inc(f_rs[2], 1)
                T.leave(NG // 2)


_INS = ['x', 'src', 'dst', 'edge_attr_128', 'edge_type_8', 'L0_gnn_W_node', 'L0_gnn_b_node', 'L0_gnn_W_edge',
        'L0_gnn_b_edge', 'L0_gnn_W_msg', 'L0_gnn_b_msg', 'L1_gnn_W', 'L1_gnn_att_q', 'L1_gnn_att_k', 'L1_gnn_bias']


def kernel(**inputs):
    import numpy as np
    import concourse.bacc as bacc
    from concourse.bass_utils import run_bass_kernel_spmd

    nc = bacc.Bacc("TRN2", target_bir_lowering=False, num_devices=1)
    arrays, args = {}, []
    for name in _INS:
        a = np.ascontiguousarray(inputs[name])
        arrays[f"in_{name}"] = a
        args.append(nc.dram_tensor(f"in_{name}", a.shape, mybir.dt.from_np(a.dtype), kind="ExternalInput").ap())
    args.append(nc.dram_tensor("out_0", inputs["x"].shape, F32, kind="ExternalOutput").ap())
    graph_layers(nc, *args)
    r = run_bass_kernel_spmd(nc, [arrays], core_ids=[0])
    return r.results[0]["out_0"]
```

```python
from contextlib import ExitStack

import concourse.bass as bass
from concourse import mybir

ALU = mybir.AluOpType
ACT = mybir.ActivationFunctionType
AX = mybir.AxisListType
F32 = mybir.dt.float32
BF16 = mybir.dt.bfloat16
I32 = mybir.dt.int32
U8 = mybir.dt.uint8

P = 128
EPS = 1e-5
SLOPE = 0.2
BIG = 1.0e30
SKIP = 1.0e6
G = 7
LOOP_A, LOOP_M, LOOP_F0, LOOP_F = 116, 72, 52, (26, 54)


class Tally:

    def __init__(self, eng, sem):
        self.eng, self.sem, self.base, self.turn, self.per, self.k = eng, sem, 0, None, 0, 0

    def of(self, ins):
        ins.then_inc(self.sem, 1)
        self.k += 1
        return ins

    def wait(self):
        n = self.base + self.k
        self.eng.wait_ge(self.sem, n if self.turn is None else self.turn * self.per + n)

    def step(self, ins):
        self.of(ins)
        self.wait()

    def enter(self, turn, per):
        self.base, self.k, self.turn, self.per = self.base + self.k, 0, turn, per

    def leave(self, turns):
        assert self.k == self.per, (self.k, self.per)
        self.base, self.k, self.turn = self.base + self.per * turns, 0, None


def graph_layers(nc, x, src, dst, ea, typ, w_node, b_node, w_edge, b_edge, w_msg, b_msg, w_rel, att_q,
                 att_k, bias, out):
    N, D = x.shape
    E = src.shape[0]
    R = w_rel.shape[1]
    TL = -(-E // P)
    TL += -TL % G
    NG = TL // G
    EP = P * TL
    FULL = E // TL
    REST = E - FULL * TL
    assert D == P and FULL == P - 1 and 0 < REST < TL and TL <= P
    BR = 6
    BC = N // P // BR
    BREM = N - BC * BR * P
    assert BREM <= P and (N // P) % BR == 0
    SLOTS = 4
    K_A = BC + 1 - 4 * NG
    K_M = [K_A + 2 * NG, K_A + 3 * NG]
    assert K_A > 0 and NG % 2 == 0
    GD = G * D

    x1_table = nc.dram_tensor("x1_table", (EP, D), F32).ap()
    h1_table = nc.dram_tensor("h1_table", (EP, D), F32).ap()
    src_cols = nc.dram_tensor("src_cols", (TL, P), F32).ap()
    typ_cols = nc.dram_tensor("typ_cols", (TL, P), U8).ap()

    with ExitStack() as ctx:
        def sb(name, shape, dt=F32):
            return ctx.enter_context(nc.sbuf_tensor(name, shape, dt))

        def sem(name):
            return ctx.enter_context(nc.semaphore(name))

        xs = sb("xs", [P, TL, D])
        ysz = sb("ysz", [P, TL + 1, D])
        xd = sb("xd", [P, TL, D])
        work = sb("work", [P, 2, GD])
        stage = sb("stage", [P, SLOTS * BR * D])
        mats = sb("mats", [P, TL * R])
        hot = sb("hot", [P, TL, R], U8)
        tmpk = sb("tmpk", [P, G, R])
        opT = sb("opT", [P, 2, GD])
        typB = sb("typB", [P, TL, P], U8)
        wr = sb("wr", [P, R, D])
        identS = sb("identS", [P, P + 2])
        ones = sb("ones", [P, P])
        carryF = sb("carryF", [P, P])
        carryB = sb("carryB", [P, P])
        bias_row = sb("bias_row", [P, 2, P])
        relu_row = sb("relu_row", [P, 2, P])
        turn = sb("turn", [P, P + 1])
        far = sb("far", [P, P])
        carry = turn[:, 0:P]
        wqk = sb("wqk", [P, 2, R, 2])
        qk = sb("qk", [P, 2, 2])
        bcol = sb("bcol", [P, 4])
        tick = sb("tick", [P, 1])
        first = sb("first", [P, 1])
        epsc = sb("epsc", [P, 1])
        srcI = sb("srcI", [P, TL], I32)
        dstI = sb("dstI", [P, TL], I32)
        dstG = sb("dstG", [P, TL], I32)
        outI = sb("outI", [P, TL], I32)
        posI = sb("posI", [P, TL], I32)
        cols = {n: sb("c_" + n, [P, TL]) for n in
                ("same", "next", "pre", "suf", "rcp", "typ", "src1", "lg", "fm", "m", "t0")}
        colbf = sb("colbf", [P, 2, TL + 1], BF16)
        st = sb("st", [P, 2, 2 * BR, 6])
        sm = sb("sm", [P, 2, 2 * BR, 2])
        df = sb("df", [P, 2, 2 * BR])
        sd = sb("sd", [P, 2, 2 * BR])
        rs = sb("rs", [P, 2, 2 * BR])
        nm = sb("nm", [P, 2, 2 * BR])
        st7 = sb("st7", [P, G, 6])
        sm7 = sb("sm7", [P, G, 2])
        df7 = sb("df7", [P, G])
        sd7 = sb("sd7", [P, G])
        rs7 = sb("rs7", [P, 2, G])
        nm7 = sb("nm7", [P, 2, G])

        ps_y = ctx.enter_context(nc.psum_tensor("ps_y", [P, 2, 1024], F32))
        ps_t = ctx.enter_context(nc.psum_tensor("ps_t", [P, 1024], F32))
        ps_k = ctx.enter_context(nc.psum_tensor("ps_k", [P, 512], F32))
        ps_s = ctx.enter_context(nc.psum_tensor("ps_s", [P, 512], F32))

        ident = identS[:, 1:P + 1]
        ys = ysz[:, 1:TL + 1, :]
        same, nxt, pre, suf, rcp = (cols[n] for n in ("same", "next", "pre", "suf", "rcp"))
        typF, src1, lg, fm, mx, t0 = (cols[n] for n in ("typ", "src1", "lg", "fm", "m", "t0"))
        scr = xd[:, 0:16, :].rearrange("p a b -> p (a b)")
        prevI, nextI, typI, aboveI, diffI, lowI, dstF, srcF = (
            scr[:, j * P:j * P + TL].bitcast(I32) if j < 6 else scr[:, j * P:j * P + TL] for j in range(8))
        diags = scr[:, 8 * P:10 * P]
        spread = xd[:, 52:55, :].rearrange("p a b -> p (a b)")
        w_sm = scr[:, 10 * P:13 * P].rearrange("p (a b) -> p a b", a=3)
        w_mT = scr[:, 13 * P:14 * P]
        b_rep = scr[:, 14 * P:15 * P]
        bm_row = scr[:, 15 * P:16 * P]
        colsT = xd[:, 16:18, :].rearrange("p a b -> p (a b)")
        typT8 = xd[:, 18, 0:P // 4].bitcast(U8)
        wT = xd[:, 20:36, :]
        w_all = xd[:, 36:52, :]
        m_node, m_edge, c_row, sel0 = (mats[:, n * P:(n + 1) * P] for n in range(4))
        q8 = mats[:].rearrange("p (t r) -> p t r", r=R)
        srcB = work[:, 0, :]
        stepT = work[:, 1, 0:GD // 2].bitcast(BF16)
        hits = work[:, 1, GD // 2:GD // 2 + G * TL // 2].bitcast(BF16).rearrange("p (t c) -> p t c", c=TL)

        def slot(c):
            b = c % SLOTS
            return stage[:, b * BR * D:(b + 1) * BR * D].rearrange("p (r d) -> p r d", d=D)

        def grp(t, g):
            return t[:, bass.ds(g * G, G), :] if not isinstance(g, int) else t[:, g * G:g * G + G, :]

        def grpc(t, g):
            return t[:, bass.ds(g * G, G)] if not isinstance(g, int) else t[:, g * G:g * G + G]

        def row_of(t, c):
            return t[:, bass.ds(c, 1), :].rearrange("p a d -> p (a d)") if not isinstance(c, int) else t[:, c, :]

        def at(t, c):
            return t[:, bass.ds(c, 1)] if not isinstance(c, int) else t[:, c:c + 1]

        def wide(ap, n):
            return ap.unsqueeze(2).to_broadcast([ap.shape[0], ap.shape[1], n])

        def mid(ap, n):
            return ap.unsqueeze(1).to_broadcast([ap.shape[0], n, ap.shape[1]])

        idx_in = sem("idx_in"); par_in = sem("par_in"); ea_in = sem("ea_in"); w0_in = sem("w0_in"); w1_in = sem("w1_in")
        cols_out = sem("cols_out"); typB_in = sem("typB_in"); srcB_in = sem("srcB_in")
        bulk_in = [sem(f"bulk_in{b}") for b in range(SLOTS)]
        bulk_out = [sem(f"bulk_out{b}") for b in range(SLOTS)]
        xs_in = [[sem(f"xs_in{j}{u}") for u in range(2)] for j in range(3)]
        xd_in = [sem(f"xd_in{u}") for u in range(2)]
        tab_out = [[sem(f"tab_out{j}{u}") for u in range(2)] for j in range(2)]
        rows_out = sem("rows_out")
        consts = sem("consts"); fills = sem("fills"); idx_f = sem("idx_f"); idx_T = sem("idx_T"); idx_Tsb = sem("idx_Tsb")
        diag_r = sem("diag_r"); diag_p = sem("diag_p")
        wmT_p = sem("wmT_p"); wmT_s = sem("wmT_s"); wrT_p = sem("wrT_p"); wrT_s = sem("wrT_s")
        brep_r = sem("brep_r"); mix_p = sem("mix_p"); mix_s = sem("mix_s"); c_r = sem("c_r"); wqk_p = sem("wqk_p"); wqk_s = sem("wqk_s")
        prol_d = sem("prol_d")
        pro = sem("dve_steps")
        b_sum = sem("b_sum"); b_sd = sem("b_sd"); b_rs = sem("b_rs"); b_norm1 = sem("b_norm1"); b_norm2 = sem("b_norm2")
        a_T = sem("a_T"); a_Ts = sem("a_Ts"); a_msg = sem("a_msg"); a_ys = sem("a_ys")
        a_sum = sem("a_sum"); a_sd = sem("a_sd"); a_rs = sem("a_rs"); a_norm = sem("a_norm"); a_scan = sem("a_scan")
        p_step = sem("p_step"); p_row = sem("p_row"); p_ready = sem("p_ready")
        cy_in = sem("cy_in"); cy_ps = sem("cy_ps")
        f_sum = [sem(f"f_sum{j}") for j in range(3)]; f_sd = [sem(f"f_sd{j}") for j in range(3)]
        f_rs = [sem(f"f_rs{j}") for j in range(3)]; f_rows = [sem(f"f_rows{j}") for j in range(3)]
        f_T = [sem(f"f_T{j}") for j in range(2)]; f_Ts = [sem(f"f_Ts{j}") for j in range(2)]
        f_q = [sem(f"f_q{j}") for j in range(2)]; f_qs = [sem(f"f_qs{j}") for j in range(2)]
        m_T = [sem(f"m_T{j}") for j in range(2)]; m_Ts = [sem(f"m_Ts{j}") for j in range(2)]
        m_k = [sem(f"m_k{j}") for j in range(2)]; m_ks = [sem(f"m_ks{j}") for j in range(2)]
        m_mask = [sem(f"m_mask{j}") for j in range(2)]; m_used = [sem(f"m_used{j}") for j in range(2)]
        m_ys = [sem(f"m_ys{j}") for j in range(2)]
        s_arg = [sem(f"s_arg{j}") for j in range(2)]; s_exp = [sem(f"s_exp{j}") for j in range(2)]
        n_y = [sem(f"n_y{j}") for j in range(2)]
        refill = sem("refill")

        x_bulk = x[0:BC * BR * P].rearrange("(p r) d -> p r d", p=P)
        o_bulk = out[0:BC * BR * P].rearrange("(p r) d -> p r d", p=P)
        x1_rows = x1_table.rearrange("(p t) d -> p t d", p=P)
        h1_rows = h1_table.rearrange("(p t) d -> p t d", p=P)
        tables = [(x1_table, x1_rows), (h1_table, h1_rows)]

        def flat(v, a, n):
            return v[a:a + n]

        def load_cols(eng, dest, v, s):
            eng.dma_start(dest[0:FULL, :], v[0:FULL * TL].rearrange("(p t) -> p t", t=TL)).then_inc(s, 16)
            eng.dma_start(dest[FULL:P, 0:REST], v[FULL * TL:E].rearrange("(a t) -> a t", a=1)).then_inc(s, 16)

        N_IDX = 14
        N_PAR = 13

        block = ctx.enter_context(nc.Block())

        @block.sync
        def _(sp):
            load_cols(sp, srcI, src, idx_in)
            sp.dma_start(srcI[FULL:P, REST:TL], src[0:TL - REST].rearrange("(a t) -> a t", a=1)).then_inc(idx_in, 16)
            load_cols(sp, typI, typ, idx_in)
            sp.dma_start(typI[FULL:P, REST:TL], typ[0:TL - REST].rearrange("(a t) -> a t", a=1)).then_inc(idx_in, 16)
            sp.wait_ge(fills, 4)
            load_cols(sp, dstI, dst, idx_in)
            sp.dma_start(prevI[0:1, 1:TL], dst[0:TL - 1].rearrange("(a t) -> a t", a=1)).then_inc(idx_in, 16)
            sp.dma_start(prevI[1:FULL, :], dst[TL - 1:FULL * TL - 1].rearrange("(p t) -> p t", t=TL)).then_inc(idx_in, 16)
            sp.dma_start(prevI[FULL:P, 0:REST], dst[FULL * TL - 1:E - 1].rearrange("(a t) -> a t", a=1)).then_inc(idx_in, 16)
            sp.dma_start(nextI[0:FULL, :], dst[1:FULL * TL + 1].rearrange("(p t) -> p t", t=TL)).then_inc(idx_in, 16)
            sp.dma_start(nextI[FULL:P, 0:REST - 1], dst[FULL * TL + 1:E].rearrange("(a t) -> a t", a=1)).then_inc(idx_in, 16)
            sp.dma_start(aboveI[1:P, :], dst[0:FULL * TL].rearrange("(p t) -> p t", t=TL)).then_inc(idx_in, 16)
            sp.dma_start(w_sm[:, 0, :], w_msg).then_inc(par_in, 16)
            sp.dma_start(w_sm[:, 1, :], w_node).then_inc(par_in, 16)
            sp.dma_start(w_sm[:, 2, :], w_edge).then_inc(par_in, 16)
            sp.dma_start(bcol[:, 0:1], b_node.unsqueeze(1)).then_inc(par_in, 16)
            sp.dma_start(bcol[:, 1:2], b_edge.unsqueeze(1)).then_inc(par_in, 16)
            sp.dma_start(bm_row, b_msg.unsqueeze(0).to_broadcast([P, D])).then_inc(par_in, 16)
            sp.dma_start(bias_row[:, 0, :], bias[0:1, :].to_broadcast([P, D])).then_inc(par_in, 16)
            sp.dma_start(bias_row[:, 1, :], bias[1:2, :].to_broadcast([P, D])).then_inc(par_in, 16)
            for j in range(2):
                sp.dma_start(qk[:, j, 0:1], att_q[j]).then_inc(par_in, 16)
                sp.dma_start(qk[:, j, 1:2], att_k[j]).then_inc(par_in, 16)
            sp.dma_start(w_all, w_rel.rearrange("l r f g -> f (l r) g")).then_inc(par_in, 16)
            sp.dma_start(wr[:], w_rel[0].rearrange("r f g -> f r g")).then_inc(w0_in, 16)
            sp.dma_start(ys[0:FULL, :, :], ea[0:FULL * TL].rearrange("(p t) d -> p t d", t=TL)).then_inc(ea_in, 16)
            sp.dma_start(ys[FULL:P, 0:REST, :], ea[FULL * TL:E].unsqueeze(0)).then_inc(ea_in, 16)
            sp.dma_start(ys[FULL:P, REST:TL, :], ea[0:TL - REST].unsqueeze(0)).then_inc(ea_in, 16)
            for c in range(SLOTS):
                sp.dma_start(slot(c), x_bulk[:, c * BR:(c + 1) * BR, :]).then_inc(bulk_in[c], 16)
            sp.wait_ge(idx_Tsb, 2)
            sp.dma_start(src_cols, colsT[0:TL, 0:P]).then_inc(cols_out, 16)
            sp.dma_start(typ_cols, typT8[0:TL, :]).then_inc(cols_out, 16)
            sp.wait_ge(cols_out, 32)
            sp.dma_start(typB[:].rearrange("p t q -> p (t q)"),
                         typ_cols.rearrange("t q -> (t q)").unsqueeze(0).to_broadcast([P, EP])).then_inc(typB_in, 16)
            src_flat = src_cols.rearrange("t q -> (t q)").unsqueeze(0)
            def src_spread(g):
                part = src_flat[:, g * G * P:(g + 1) * G * P] if isinstance(g, int) else src_flat[:, bass.ds(g * (G * P), G * P)]
                sp.dma_start(srcB, part.to_broadcast([P, G * P])).then_inc(srcB_in, 16)

            src_spread(0)

            def bulk_step(k, kb):
                b = (kb - 1) % SLOTS
                sp.wait_ge(b_norm2, k)
                sp.dma_start(o_bulk[:, bass.ds((k - 1) * BR, BR), :] if not isinstance(k, int) else
                             o_bulk[:, (k - 1) * BR:k * BR, :], slot(b)).then_inc(bulk_out[b], 16)
                if isinstance(k, int) and k + SLOTS - 1 > BC:
                    return
                sp.wait_ge(bulk_out[b], (k - 1 - b) * (16 // SLOTS) + 16)
                if isinstance(k, int) and k + SLOTS - 1 == BC:
                    sp.dma_start(slot(b)[0:BREM, 0, :], x[BC * BR * P:N]).then_inc(bulk_in[b], 16)
                    return
                c = k + SLOTS - 1
                sp.dma_start(slot(b), x_bulk[:, bass.ds(c * BR, BR), :] if not isinstance(k, int) else
                             x_bulk[:, c * BR:(c + 1) * BR, :]).then_inc(bulk_in[b], 16)

            def bulk_steps(k0, n):
                turns = (n - SLOTS - 1) // SLOTS if k0 + n > BC - SLOTS else n // SLOTS
                with sp.Fori(0, turns) as i:
                    for q in range(SLOTS):
                        bulk_step(i * SLOTS + (k0 + q), (k0 + q) % SLOTS)
                for k in range(k0 + turns * SLOTS, k0 + n):
                    bulk_step(k, k % SLOTS)

            for k in range(1, K_A):
                bulk_step(k, k % SLOTS)
            with sp.Fori(0, NG // 2 - 1) as i:
                for u in range(2):
                    sp.wait_ge(p_step, i * 2 + (u + 1))
                    src_spread(i * 2 + (u + 1))
                    for q in range(2 * u, 2 * u + 2):
                        bulk_step(i * SLOTS + (K_A + q), (K_A + q) % SLOTS)
            sp.wait_ge(p_step, NG - 1)
            src_spread(NG - 1)
            for k in range(K_A + 2 * NG - SLOTS, K_A + 2 * NG):
                bulk_step(k, k % SLOTS)

            for j in range(2):
                rows, buf = tables[j][1], (xd, ys)[j]
                if j == 1:
                    sp.wait_ge(m_used[0], NG * R + 2)
                    sp.dma_start(wr[:], w_rel[1].rearrange("r f g -> f r g")).then_inc(w1_in, 16)
                with sp.Fori(0, NG // 2) as i:
                    for u in range(2):
                        sp.wait_ge(f_rows[j], i * 2 + (u + 1))
                        sp.dma_start(grp(rows, i * 2 + u), grp(buf, i * 2 + u)).then_inc(tab_out[j][u], 16)
                bulk_steps(K_M[j], NG)
            sp.wait_ge(b_norm2, BC + 1)
            sp.dma_start(out[BC * BR * P:N], slot(BC)[0:BREM, 0, :]).then_inc(bulk_out[BC % SLOTS], 16)

        @block.gpsimd
        def _(pool):
            nc.gpsimd.memset(prevI, -1).then_inc(fills, 1)
            nc.gpsimd.memset(nextI, -1).then_inc(fills, 1)
            nc.gpsimd.memset(aboveI, -1).then_inc(fills, 1)
            nc.gpsimd.memset(dstI[:], N).then_inc(fills, 1)
            nc.gpsimd.memset(ones[:], 1.0).then_inc(consts, 1)
            nc.gpsimd.memset(epsc[:], EPS).then_inc(consts, 1)
            nc.gpsimd.memset(identS[:], 0.0).then_inc(consts, 1)
            nc.gpsimd.memset(sel0, 0.0).then_inc(consts, 1)
            nc.gpsimd.memset(turn[:], 0.0).then_inc(consts, 1)
            pool.wait_ge(consts, 5)
            nc.gpsimd.affine_select(out=identS[:], in_=identS[:], compare_op=ALU.not_equal, fill=1.0, base=1,
                                    pattern=[[-1, P + 2]], channel_multiplier=1).then_inc(consts, 1)
            nc.gpsimd.affine_select(out=sel0, in_=sel0, compare_op=ALU.not_equal, fill=1.0, base=0,
                                    pattern=[[0, P]], channel_multiplier=1).then_inc(consts, 1)

            def gather(buf, table, idx, sems, bound, ready=None):
                for g in range(NG):
                    u = g % 2
                    if g >= 2:
                        pool.wait_ge(sems[u], 16 * G * (g // 2))
                    if ready:
                        pool.wait_ge(ready, g + 1)
                    for t in range(g * G, g * G + G):
                        extra = {} if bound is None else dict(bounds_check=bound, oob_is_err=False)
                        nc.gpsimd.indirect_dma_start(
                            out=buf[:, t, :], out_offset=None, in_=table,
                            in_offset=bass.IndirectOffsetOnAxis(ap=idx[:, t:t + 1], axis=0), **extra).then_inc(sems[u], 16)

            pool.wait_ge(idx_in, 16 * N_IDX)
            gather(xs, x, srcI, xs_in[0], None)
            pool.wait_ge(prol_d, 1)
            pool.wait_ge(cols_out, 32)
            pool.wait_ge(mix_s, 2)
            pool.wait_ge(wqk_p, 1)
            gather(xd, x, dstG, xd_in, None)
            for j in range(2):
                pool.wait_ge(p_ready, 1)
                if j == 1:
                    for g in range(NG):
                        pool.wait_ge(m_T[0], g + 1)
                        nc.gpsimd.tensor_copy(grp(xs, g), mid(relu_row[:, 0, :], G)).then_inc(refill, 1)
                for u in range(2):
                    pool.wait_ge(tab_out[j][u], 16 * NG // 2)
                gather(xs, tables[j][0], posI, xs_in[j + 1], EP - 1, ready=(a_norm, refill)[j])
            for b in range(SLOTS):
                pool.wait_ge(bulk_out[b], 16 * len(range(b, BC + 1, SLOTS)))
            for g in range(NG):
                pool.wait_ge(f_rows[2], g + 1)
                for t in range(g * G, g * G + G):
                    nc.gpsimd.indirect_dma_start(
                        out=out, out_offset=bass.IndirectOffsetOnAxis(ap=outI[:, t:t + 1], axis=0),
                        in_=xd[:, t, :], in_offset=None, bounds_check=N - 1, oob_is_err=False).then_inc(rows_out, 16)
            pool.wait_ge(rows_out, 16 * TL)

        @block.tensor
        def _(pe):
            pe.wait_ge(consts, 7)
            pe.wait_ge(idx_f, 1)
            pe.transpose(ps_s[0:TL, 0:P], srcF, ident)
            pe.transpose(ps_s[0:TL, P:2 * P], typF[:], ident).then_inc(idx_T, 1)
            pe.wait_ge(par_in, 16 * N_PAR)
            pe.transpose(ps_t[:, 0:P], w_sm[:, 0, :], ident).then_inc(wmT_p, 1)
            for a in range(2 * R):
                mm = pe.transpose(ps_y[:, a // R, a % R * P:(a % R + 1) * P], w_all[:, a, :], ident)
            mm.then_inc(wrT_p, 1)
            pe.wait_ge(diag_r, 1)
            pe.wait_ge(idx_Tsb, 2)
            pe.matmul(ps_s[:, 2 * P:4 * P], ones[:], diags, start=True, stop=True).then_inc(diag_p, 1)
            pe.wait_ge(wmT_s, 1)
            pe.matmul(ps_t[:, P:2 * P], w_sm[:, 1, :], w_mT, start=True, stop=True)
            pe.matmul(ps_t[:, 2 * P:3 * P], w_sm[:, 2, :], w_mT, start=True, stop=True)
            pe.wait_ge(brep_r, 1)
            pe.matmul(ps_t[:, 3 * P:4 * P], b_rep, w_mT, start=True, stop=True).then_inc(mix_p, 1)
            pe.wait_ge(wrT_s, 1)
            for a in range(2 * R):
                mm = pe.matmul(ps_k[:, 2 * a:2 * a + 2], wT[:, a, :], qk[:, a // R, :], start=True, stop=True)
            mm.then_inc(wqk_p, 1)

            pe.wait_ge(mix_s, 2)
            pe.wait_ge(c_r, 1)
            pe.wait_ge(ea_in, 48)
            for g in range(NG):
                pe.wait_ge(p_step, g + 1)
                for t in range(G):
                    o = ps_y[:, 1, t * P:t * P + TL + 1]
                    pe.matmul(o, stepT[:, t * P:(t + 1) * P], colbf[:, 0, :], start=True, stop=False)
                    mm = pe.matmul(o, stepT[:, t * P:(t + 1) * P], colbf[:, 1, :], start=False, stop=True)
                mm.then_inc(p_row, 1)
                u = g % 2
                pe.wait_ge(xs_in[0][u], (g // 2 + 1) * (16 * G))
                pe.wait_ge(a_Ts, g * 2 + 1)
                for t in range(G):
                    mm = pe.transpose(ps_t[:, t * P:(t + 1) * P], row_of(xs, g * G + t), ident)
                mm.then_inc(a_T, 1)
                pe.wait_ge(a_Ts, g * 2 + 2)
                for t in range(G):
                    mm = pe.transpose(ps_t[:, t * P:(t + 1) * P], row_of(ys, g * G + t), ident)
                mm.then_inc(a_T, 1)
                pe.wait_ge(a_Ts, g * 2 + 3)
                pe.wait_ge(a_ys, g + 1)
                for t in range(G):
                    o = ps_y[:, 0, t * P:(t + 1) * P]
                    pe.matmul(o, opT[:, 0, t * P:(t + 1) * P], m_node, start=True, stop=False)
                    pe.matmul(o, opT[:, 1, t * P:(t + 1) * P], m_edge, start=False, stop=False)
                    mm = pe.matmul(o, sel0, c_row, start=False, stop=True)
                mm.then_inc(a_msg, 1)

            uses = [0]

            def carry_product(mat, rhs, n):
                uses[0] += 1
                pe.wait_ge(cy_in, uses[0])
                pe.matmul(ps_s[:, 0:n], mat, rhs, start=True, stop=True).then_inc(cy_ps, 1)

            def carry_turn():
                uses[0] += 1
                pe.wait_ge(cy_in, uses[0])
                pe.transpose(ps_s[:, 0:P], turn[:, 0:P], ident).then_inc(cy_ps, 1)

            def node_scores(j):
                buf = (xd, ys)[j]
                for g in range(NG):
                    u = g % 2
                    pe.wait_ge(f_rows[j], g + 1)
                    pe.wait_ge(f_Ts[j], g + 1)
                    for t in range(G):
                        mm = pe.transpose(ps_t[:, t * P:(t + 1) * P], row_of(buf, g * G + t), ident)
                    mm.then_inc(f_T[j], 1)
                    pe.wait_ge(f_Ts[j], g + 2)
                    pe.wait_ge(f_qs[j], g + 1)
                    for t in range(G):
                        mm = pe.matmul(ps_k[:, t * R:(t + 1) * R], opT[:, u, t * P:(t + 1) * P], wqk[:, j, :, 0],
                                       start=True, stop=True)
                    mm.then_inc(f_q[j], 1)

            def relation_products(j):
                pe.wait_ge((w0_in, w1_in)[j], 16)

                def turn_rows(g, u, rows_in):
                    pe.wait_ge(xs_in[j + 1][u], rows_in)
                    pe.wait_ge(m_Ts[j], g + 1)
                    for t in range(G):
                        mm = pe.transpose(ps_t[:, t * P:(t + 1) * P], row_of(xs, g * G + t), ident)
                    mm.then_inc(m_T[j], 1)

                def key_scores(g, u):
                    pe.wait_ge(m_Ts[j], g + 2)
                    pe.wait_ge(m_ks[j], g + 1)
                    for t in range(G):
                        mm = pe.matmul(ps_k[:, t * R:(t + 1) * R], opT[:, u, t * P:(t + 1) * P],
                                       wqk[:, j, :, 1], start=True, stop=True)
                    mm.then_inc(m_k[j], 1)

                def products(g, u):
                    pe.wait_ge(m_ys[j], g + 1)
                    for r in range(R):
                        pe.wait_ge(m_mask[j], g * R + (r + 1 + 2 * R))
                        for t in range(G):
                            mm = pe.matmul(ps_y[:, u, t * P:(t + 1) * P], work[:, r % 2, t * P:(t + 1) * P],
                                           wr[:, r, :], start=(r == 0 and t % 4 == 0), stop=(r == R - 1),
                                           skip_group_check=True)
                        mm.then_inc(m_used[j], 1)

                pe.sem_inc(m_used[j], 2)
                turn_rows(0, 0, 16 * G)
                key_scores(0, 0)
                for g in range(NG):
                    u = g % 2
                    if g < NG - 1:
                        turn_rows(g + 1, 1 - u, ((g + 1) // 2 + 1) * (16 * G))
                    products(g, u)
                    if g < NG - 1:
                        key_scores(g + 1, 1 - u)

            carry_product(carryF[:], t0[:, TL - 1:TL], 1)
            carry_product(carryF[:], ys[:, TL - 1, :], P)
            node_scores(0)
            for j in range(2):
                carry_product(carryB[:], q8[:, 0, :], R)
                relation_products(j)
                carry_turn()
                carry_turn()
                carry_product(carryB[:], mx[:, 0:1], 1)
                carry_product(carryF[:], fm[:, TL - 1:TL], 1)
                carry_product(carryF[:], ys[:, TL - 1, :], P)
                if j == 0:
                    node_scores(1)

        @block.scalar
        def _(act):
            a = nc.scalar

            def copy(o, i_):
                return a.activation(o, i_, ACT.Copy)

            act.sem_inc(a_Ts, 1)
            act.sem_inc(a_ys, 1)
            for j in range(2):
                act.sem_inc(f_qs[j], 1)
                act.sem_inc(f_Ts[j], 1)
                act.sem_inc(m_Ts[j], 1)
                act.sem_inc(m_ys[j], 2)
            act.wait_ge(idx_T, 1)
            copy(colsT[0:TL, 0:P], ps_s[0:TL, 0:P]).then_inc(idx_Tsb, 1)
            copy(typT8[0:TL, :], ps_s[0:TL, P:2 * P]).then_inc(idx_Tsb, 1)
            act.wait_ge(wmT_p, 1)
            copy(w_mT, ps_t[:, 0:P]).then_inc(wmT_s, 1)
            act.wait_ge(wrT_p, 1)
            copy(wT[:, 0:R, :], ps_y[:, 0, :].rearrange("p (a b) -> p a b", b=P))
            copy(wT[:, R:2 * R, :], ps_y[:, 1, :].rearrange("p (a b) -> p a b", b=P)).then_inc(wrT_s, 1)
            act.wait_ge(mix_p, 1)
            copy(m_node, ps_t[:, P:2 * P]).then_inc(mix_s, 1)
            copy(m_edge, ps_t[:, 2 * P:3 * P]).then_inc(mix_s, 1)
            act.wait_ge(wqk_p, 1)
            copy(wqk[:].rearrange("p l r a -> p (l r a)"), ps_k[:, 0:4 * R]).then_inc(wqk_s, 1)

            def bulk_sd(k, kb, first=True, second=True):
                h, lo, hi = kb % 2, 0 if first else BR, 2 * BR if second else BR
                act.wait_ge(b_sum, k + 1)
                a.activation(sd[:, h, lo:hi], df[:, h, lo:hi], ACT.Sqrt, bias=epsc[:, 0:1], scale=1.0 / D).then_inc(b_sd, 1)

            def bulk_norms(k, kb, first=True, second=True):
                h = kb % 2
                act.wait_ge(b_rs, k + 1)
                for half, c, s_ in ((0, kb, b_norm1), (1, kb - 1, b_norm2)):
                    if not (first, second)[half]:
                        continue
                    for r in range(BR):
                        n = half * BR + r
                        ins = a.activation(slot(c)[:, r, :], slot(c)[:, r, :], ACT.Identity,
                                           bias=nm[:, h, n:n + 1], scale=rs[:, h, n:n + 1])
                    ins.then_inc(s_, 1)

            def bulk_step(k, kb, first=True, second=True):
                bulk_sd(k, kb, first, second)
                bulk_norms(k, kb, first, second)

            def out_of_psum(o, i_, producer, n, done):
                act.wait_ge(producer, n)
                copy(o, i_).then_inc(done, 1)

            bulk_step(0, 0, second=False)
            for k in range(1, K_A):
                bulk_step(k, k % SLOTS)
            with act.Fori(0, NG // 2) as i:
                for u in range(2):
                    g = i * 2 + u
                    kA, kB = (i * SLOTS + (K_A + 2 * u + q) for q in range(2))
                    bA, bB = ((K_A + 2 * u + q) % SLOTS for q in range(2))
                    out_of_psum(opT[:, 0, :], ps_t[:, 0:GD], a_T, g * 2 + 1, a_Ts)
                    bulk_sd(kA, bA)
                    out_of_psum(opT[:, 1, :], ps_t[:, 0:GD], a_T, g * 2 + 2, a_Ts)
                    act.wait_ge(a_sum, g + 1)
                    a.activation(sd7[:], df7[:], ACT.Sqrt, bias=epsc[:, 0:1], scale=1.0 / D).then_inc(a_sd, 1)
                    bulk_norms(kA, bA)
                    out_of_psum(grp(ys, g).rearrange("p a b -> p (a b)"), ps_y[:, 0, 0:GD], a_msg, g + 1, a_ys)
                    act.wait_ge(a_rs, g + 1)
                    for t in range(G):
                        ins = a.activation(row_of(xs, g * G + t), row_of(xs, g * G + t), ACT.Identity,
                                           bias=nm7[:, u, t:t + 1], scale=rs7[:, u, t:t + 1])
                    ins.then_inc(a_norm, 1)
                    bulk_sd(kB, bB)
                    bulk_norms(kB, bB)

            def query_rows_out(j, g, u):
                out_of_psum(opT[:, u, :], ps_t[:, 0:GD], f_T[j], g + 1, f_Ts[j])

            def query_scores_out(j, g):
                out_of_psum(grp(q8, g), ps_k[:, 0:G * R].rearrange("p (t r) -> p t r", r=R), f_q[j], g + 1, f_qs[j])

            def norm_rows(j, g, u, last=None):
                act.wait_ge(f_sum[j], g + 1)
                a.activation(sd7[:], df7[:], ACT.Sqrt, bias=epsc[:, 0:1], scale=1.0 / D).then_inc(f_sd[j], 1)
                if last is not None:
                    query_rows_out(j, last, 1 - u)
                act.wait_ge(f_rs[j], g + 1)
                for t in range(G):
                    ins = a.activation(row_of(xd, g * G + t), row_of(xd, g * G + t), ACT.Identity,
                                       bias=nm7[:, u, t:t + 1], scale=rs7[:, u, t:t + 1])
                ins.then_inc(f_rows[j], 1)
                if last is not None:
                    query_scores_out(j, last)

            norm_rows(0, 0, 0)
            norm_rows(0, 1, 1, last=0)
            with act.Fori(1, NG // 2) as i:
                for u in range(2):
                    norm_rows(0, i * 2 + u, u, last=i * 2 + (u - 1))
            query_rows_out(0, NG - 1, 1)
            query_scores_out(0, NG - 1)

            for j in range(2):
                def rows_T(g, u):
                    act.wait_ge(m_mask[j], (g + 1) * R)
                    out_of_psum(opT[:, u, :], ps_t[:, 0:GD], m_T[j], g + 1, m_Ts[j])

                def products_out(g, u):
                    out_of_psum(grp(ys, g).rearrange("p a b -> p (a b)"), ps_y[:, u, 0:GD],
                                m_used[j], (g + 1) * R + 2, m_ys[j])

                def group(g, q, k):
                    rows_T(g + 1, (q + 1) % 2)
                    bulk_step(k, (K_M[j] + q) % SLOTS)
                    products_out(g, q % 2)

                rows_T(0, 0)
                with act.Fori(0, NG // SLOTS) as i:
                    for q in range(SLOTS):
                        group(i * SLOTS + q, q, i * SLOTS + (K_M[j] + q))
                for g in range(NG // SLOTS * SLOTS, NG - 1):
                    group(g, g % SLOTS, K_M[j] + g)
                bulk_step(K_M[j] + NG - 1, (K_M[j] + NG - 1) % SLOTS)
                products_out(NG - 1, 1)
                if j == 1:
                    bulk_step(BC + 1, (BC + 1) % SLOTS, first=False)
                act.wait_ge(s_arg[j], 1)
                a.activation(lg[:], lg[:], ACT.Exp).then_inc(s_exp[j], 1)
                act.wait_ge(s_exp[j], 1)
                act.wait_ge(m_ys[j], NG + 2)
                with act.Fori(0, NG) as g:
                    for t in range(G):
                        ins = a.activation(row_of(ys, g * G + t), row_of(ys, g * G + t), ACT.Copy, scale=at(lg, g * G + t))
                    ins.then_inc(n_y[j], 1)
                if j == 0:
                    def relu_rows(g, u, last=None):
                        act.wait_ge(f_sum[1], g + 1)
                        a.activation(grp(ys, g), grp(ys, g), ACT.Relu).then_inc(f_rows[1], 1)
                        if last is not None:
                            query_rows_out(1, last, 1 - u)
                            query_scores_out(1, last)

                    relu_rows(0, 0)
                    relu_rows(1, 1, last=0)
                    with act.Fori(1, NG // 2) as i:
                        for u in range(2):
                            relu_rows(i * 2 + u, u, last=i * 2 + (u - 1))
                    query_rows_out(1, NG - 1, 1)
                    query_scores_out(1, NG - 1)
                else:
                    with act.Fori(0, NG // 2) as i:
                        for u in range(2):
                            norm_rows(2, i * 2 + u, u)

        @block.vector
        def _(dve):
            v = nc.vector
            T = Tally(dve, pro)
            STT, TT, TS = v.scalar_tensor_tensor, v.tensor_tensor, v.tensor_scalar

            for j in range(2):
                dve.sem_inc(m_mask[j], 2 * R)
                dve.sem_inc(m_ks[j], 1)
            dve.wait_ge(idx_in, 16 * N_IDX)
            T.of(v.tensor_copy(srcF, srcI[:]))
            T.of(v.tensor_copy(typF[:], typI))
            T.of(v.tensor_copy(dstF, dstI[:]))
            T.of(v.tensor_copy(first[:], dstI[:, 0:1]))
            T.of(TT(same[:], dstI[:], prevI, ALU.is_equal))
            T.of(TT(nxt[:], dstI[:], nextI, ALU.is_equal))
            T.of(TS(dstG[:], dstI[:], float(N - 1), None, ALU.min))
            T.step(TT(diffI, dstI[:], aboveI, ALU.subtract))
            T.step(TS(src1[:], srcF, 1.0, None, ALU.add))
            dve.sem_inc(idx_f, 1)
            T.of(v.tensor_tensor_scan(pre[:], same[:], same[:], 1.0, ALU.mult, ALU.min))
            T.of(v.tensor_tensor_scan(suf[:, ::-1], nxt[:, ::-1], nxt[:, ::-1], 1.0, ALU.mult, ALU.min))
            T.of(STT(t0[:], nxt[:], SKIP, dstF, ALU.mult, ALU.add))
            T.of(TS(lowI, diffI, 255, None, ALU.bitwise_and))
            T.step(v.memset(colbf[:, 0, TL:TL + 1], 1.0))
            T.of(v.memset(colbf[:, 1, TL:TL + 1], 0.0))
            T.of(v.tensor_copy(outI[:], t0[:]))
            T.of(TT(colbf[:, 0, 0:TL], diffI, lowI, ALU.subtract))
            T.of(v.tensor_copy(colbf[:, 1, 0:TL], lowI))
            dve.wait_ge(consts, 7)
            T.of(TS(diags[:, 0:P], ident, pre[:, TL - 1:TL], None, ALU.mult))
            T.step(TS(diags[:, P:2 * P], ident, suf[:, 0:1], None, ALU.mult))
            dve.sem_inc(diag_r, 1)
            dve.wait_ge(par_in, 16 * N_PAR)
            T.step(TT(bcol[:, 2:3], bcol[:, 0:1], bcol[:, 1:2], ALU.add))
            T.of(TS(relu_row[:], bias_row[:], 0.0, None, ALU.max))
            T.step(TS(b_rep, ones[:], bcol[:, 2:3], None, ALU.mult))
            dve.sem_inc(brep_r, 1)
            dve.wait_ge(diag_p, 1)
            T.of(v.memset(spread[:, 0:1], 0.0))
            T.of(v.memset(spread[:, 2 * P + 1:2 * P + 2], 0.0))
            T.of(v.tensor_copy(spread[:, 1:2 * P + 1], ps_s[:, 2 * P:4 * P]))
            T.step(TS(far[0:1, :], ps_s[0:1, 2 * P:3 * P], 1.0, BIG, ALU.subtract, ALU.mult))
            T.of(v.tensor_tensor_scan(carryF[:], spread[:, 0:P], identS[:, 0:P], 0.0, ALU.mult, ALU.add))
            T.step(v.tensor_tensor_scan(carryB[:, ::-1], spread[:, P + 2:2 * P + 2][:, ::-1], identS[:, 2:P + 2][:, ::-1],
                                        0.0, ALU.mult, ALU.add))
            dve.wait_ge(mix_s, 2)
            T.step(TT(c_row, ps_t[:, 3 * P:4 * P], bm_row, ALU.add))
            dve.sem_inc(c_r, 1)
            dve.sem_inc(prol_d, 1)

            def sums(stats, s2, d):
                T.of(TT(s2, stats[:, :, 1:3], stats[:, :, 4:6], ALU.add))
                T.step(TT(d, stats[:, :, 1], stats[:, :, 4], ALU.subtract))
                T.step(STT(d, d, 32.0, d, ALU.mult, ALU.mult))
                return TT(d, d, s2[:, :, 1], ALU.add)

            def scales(dev, s2, r_, n_):
                T.step(v.reciprocal(r_, dev))
                return STT(n_, s2[:, :, 0], -0.5, r_, ALU.mult, ALU.mult)

            def bulk_first(k, kb, rows=range(BR)):
                dve.wait_ge(bulk_in[kb], (k - kb) * (16 // SLOTS) + 16)
                for r in rows:
                    T.of(v.bn_stats(st[:, kb % 2, r, :], slot(kb)[:, r, :]))

            def bulk_shift(k, kb):
                dve.wait_ge(b_norm1, k)
                T.of(TT(slot(kb - 1), slot(kb - 1), mid(relu_row[:, 1, :], BR), ALU.add))

            def bulk_second(k, kb, rows=range(BR)):
                for r in rows:
                    if r == 0:
                        T.wait()
                    T.of(v.bn_stats(st[:, kb % 2, BR + r, :], slot(kb - 1)[:, r, :]))

            def bulk_sums(k, kb, lo=0, hi=2 * BR):
                h = kb % 2
                T.wait()
                sums(st[:, h, lo:hi, :], sm[:, h, lo:hi, :], df[:, h, lo:hi]).then_inc(b_sum, 1)

            def bulk_scales(k, kb, lo=0, hi=2 * BR):
                h = kb % 2
                dve.wait_ge(b_sd, k + 1)
                scales(sd[:, h, lo:hi], sm[:, h, lo:hi, :], rs[:, h, lo:hi], nm[:, h, lo:hi]).then_inc(b_rs, 1)

            def bulk_statistics(k, kb, first=True, second=True):
                if first:
                    bulk_first(k, kb)
                if second:
                    bulk_shift(k, kb)
                    bulk_second(k, kb)
                bulk_sums(k, kb, 0 if first else BR, 2 * BR if second else BR)

            def bulk_step(k, kb, first=True, second=True):
                bulk_statistics(k, kb, first, second)
                bulk_scales(k, kb, 0 if first else BR, 2 * BR if second else BR)

            def bulk_piece(n, k, kb):
                if n < 2:
                    bulk_first(k, kb, range(n * BR // 2, (n + 1) * BR // 2))
                elif n == 2:
                    bulk_shift(k, kb)
                elif n < 5:
                    bulk_second(k, kb, range((n - 3) * BR // 2, (n - 2) * BR // 2))
                elif n == 5:
                    bulk_sums(k, kb)
                elif n == 7:
                    bulk_scales(k, kb)

            def scan_rows(g):
                for t in range(G):
                    c = g * G + t
                    T.step(STT(row_of(ys, c), row_of(ysz, c), at(same, c), row_of(ys, c), ALU.mult, ALU.add))

            def stats7(buf, g):
                T.of(v.memset(tick[:], 0.0))
                for t in range(G):
                    T.of(v.bn_stats(st7[:, t, :], row_of(buf, g * G + t)))
                T.wait()

            T.step(v.memset(ysz[:, 0, :], 0.0))
            bulk_step(0, 0, second=False)
            for k in range(1, K_A):
                bulk_step(k, k % SLOTS)

            def search(g):
                dve.wait_ge(p_row, g + 1)
                rows = ps_y[:, 1, :].rearrange("p (t c) -> p t c", c=P)[:, 0:G, :]
                mine = wide(grpc(src1, g), TL)
                T.of(TS(grpc(mx, g), rows[:, :, TL], float(TL), None, ALU.mult))
                T.step(TT(hits, rows[:, :, 0:TL], mine, ALU.is_le))
                T.step(v.tensor_reduce(grpc(fm, g), hits, AX.X, ALU.add))
                T.step(TT(hits, rows[:, :, 0:TL], mine, ALU.is_equal))
                T.step(v.tensor_reduce(grpc(lg, g), hits, AX.X, ALU.max))

            for r in range(R):
                T.of(TS(hot[:, :, r], typF[:], float(r), None, ALU.is_equal))
            with dve.Fori(0, NG // 2) as i:
                T.enter(i, LOOP_A)
                for u in range(2):
                    g = i * 2 + u
                    dve.wait_ge(srcB_in, i * 32 + (16 * u + 16))
                    TS(stepT, srcB, first[:, 0:1], None, ALU.is_ge).then_inc(p_step, 1)
                    kA, kB = (i * SLOTS + (K_A + 2 * u + q) for q in range(2))
                    bA, bB = ((K_A + 2 * u + q) % SLOTS for q in range(2))
                    bulk_statistics(kA, bA)
                    dve.wait_ge(xs_in[0][u], i * (16 * G) + 16 * G)
                    stats7(xs, g)
                    sums(st7[:], sm7[:], df7[:]).then_inc(a_sum, 1)
                    bulk_scales(kA, bA)
                    search(g)
                    dve.wait_ge(a_sd, g + 1)
                    scales(sd7[:], sm7[:], rs7[:, u, :], nm7[:, u, :]).then_inc(a_rs, 1)
                    bulk_statistics(kB, bB)
                    dve.wait_ge(a_ys, g + 2)
                    scan_rows(g)
                    bulk_scales(kB, bB)
            T.leave(NG // 2)
            T.step(TT(fm[:], fm[:], mx[:], ALU.add))
            T.step(TS(lg[:], lg[:], -SKIP, SKIP - TL - 1.0, ALU.mult, ALU.add))
            T.step(TT(lg[:], lg[:], fm[:], ALU.add))
            T.step(v.tensor_copy(posI[:], lg[:]))
            dve.sem_inc(p_ready, 1)

            uses = [0]

            def carried():
                uses[0] += 1
                dve.sem_inc(cy_in, 1)
                dve.wait_ge(cy_ps, uses[0])

            def carried_rows():
                carried()
                T.step(v.tensor_copy(carry, ps_s[:, 0:P]))

            T.step(v.tensor_tensor_scan(t0[:], same[:], ones[:, 0:TL], 0.0, ALU.mult, ALU.add))
            carried()
            T.step(STT(t0[:], pre[:], ps_s[:, 0:1], t0[:], ALU.mult, ALU.add))
            T.step(v.reciprocal(rcp[:], t0[:]))
            carried_rows()

            def whole_sums(g):
                for t in range(G):
                    c = g * G + t
                    T.of(STT(row_of(ys, c), carry, at(pre, c), row_of(ys, c), ALU.mult, ALU.add))
                T.wait()

            with dve.Fori(0, NG // 2) as i:
                T.enter(i, LOOP_F0)
                for u in range(2):
                    g = i * 2 + u
                    whole_sums(g)
                    dve.wait_ge(xd_in[u], i * (16 * G) + 16 * G)
                    for t in range(G):
                        c = g * G + t
                        T.of(STT(row_of(xd, c), row_of(ys, c), at(rcp, c), row_of(xd, c), ALU.mult, ALU.add))
                    T.wait()
                    stats7(xd, g)
                    sums(st7[:], sm7[:], df7[:]).then_inc(f_sum[0], 1)
                    dve.wait_ge(f_sd[0], g + 1)
                    scales(sd7[:], sm7[:], rs7[:, u, :], nm7[:, u, :]).then_inc(f_rs[0], 1)
            T.leave(NG // 2)

            for j in range(2):
                dve.wait_ge(f_qs[j], NG + 1)
                T.step(TS(t0[:], nxt[:], -1.0, 1.0, ALU.mult, ALU.add))
                T.step(TT(q8, q8, wide(t0[:], R), ALU.mult))
                for r in range(R):
                    T.of(v.tensor_tensor_scan(q8[:, ::-1, r], nxt[:, ::-1], q8[:, ::-1, r], 0.0, ALU.mult, ALU.add))
                T.wait()
                carried()
                for r in range(R):
                    T.of(STT(q8[:, :, r], suf[:], ps_s[:, r:r + 1], q8[:, :, r], ALU.mult, ALU.add))
                T.wait()
                if j == 0:
                    dve.wait_ge(typB_in, 16)

                def group(g, q, k):
                    dve.wait_ge(m_Ts[j], g + 2)
                    for r in range(R):
                        dve.wait_ge(m_used[j], g * R + (r + 1))
                        STT(work[:, r % 2, :], grp(typB, g).rearrange("p a b -> p (a b)"), float(r),
                            opT[:, q % 2, :], ALU.is_equal, ALU.mult).then_inc(m_mask[j], 1)
                        bulk_piece(r, k, (K_M[j] + q) % SLOTS)
                    dve.wait_ge(m_k[j], g + 1)
                    TT(tmpk[:], ps_k[:, 0:G * R].rearrange("p (t r) -> p t r", r=R), grp(hot, g), ALU.mult).then_inc(m_ks[j], 1)
                    dve.wait_ge(m_ks[j], g + 2)
                    T.step(v.tensor_reduce(grpc(lg, g), tmpk[:], AX.X, ALU.add))

                with dve.Fori(0, NG // SLOTS) as i:
                    T.enter(i, LOOP_M)
                    for q in range(SLOTS):
                        group(i * SLOTS + q, q, i * SLOTS + (K_M[j] + q))
                T.leave(NG // SLOTS)
                for g in range(NG // SLOTS * SLOTS, NG):
                    group(g, g % SLOTS, K_M[j] + g)
                if j == 1:
                    bulk_step(BC + 1, (BC + 1) % SLOTS, first=False)
                T.step(TT(q8, q8, hot[:], ALU.mult))
                T.step(v.tensor_reduce(t0[:], q8, AX.X, ALU.add))
                T.step(TT(t0[:], t0[:], lg[:], ALU.add))
                T.step(STT(lg[:], t0[:], SLOPE, t0[:], ALU.mult, ALU.max))
                T.step(TS(t0[:], same[:], 1.0, BIG, ALU.subtract, ALU.mult))
                T.step(v.tensor_tensor_scan(fm[:], t0[:], lg[:], -BIG, ALU.add, ALU.max))
                T.step(v.tensor_copy(turn[:, 0:1], fm[:, TL - 1:TL]))
                carried()
                T.of(v.tensor_tensor_scan(turn[0:1, 1:P + 1], far[0:1, :], ps_s[0:1, 0:P], -BIG, ALU.add, ALU.max))
                T.step(v.memset(turn[0:1, 0:1], -BIG))
                carried()
                T.step(v.tensor_copy(mx[:, 0:1], ps_s[:, 0:1]))
                T.step(v.tensor_tensor_scan(fm[:], t0[:], lg[:], mx[:, 0:1], ALU.add, ALU.max))
                T.step(TT(t0[:], nxt[:], fm[:], ALU.mult))
                T.step(TT(t0[:], fm[:], t0[:], ALU.subtract))
                T.step(v.tensor_tensor_scan(mx[:, ::-1], nxt[:, ::-1], t0[:, ::-1], 0.0, ALU.mult, ALU.add))
                carried()
                T.step(STT(mx[:], suf[:], ps_s[:, 0:1], mx[:], ALU.mult, ALU.add))
                T.step(TT(lg[:], lg[:], mx[:], ALU.subtract))
                dve.sem_inc(s_arg[j], 1)
                dve.wait_ge(s_exp[j], 1)
                T.step(v.tensor_tensor_scan(fm[:], same[:], lg[:], 0.0, ALU.mult, ALU.add))
                carried()
                T.step(STT(fm[:], pre[:], ps_s[:, 0:1], fm[:], ALU.mult, ALU.add))
                T.step(TS(fm[:], fm[:], 1e-16, None, ALU.add))
                T.step(v.reciprocal(rcp[:], fm[:]))
                with dve.Fori(0, NG) as g:
                    T.enter(g, G)
                    dve.wait_ge(n_y[j], g + 1)
                    scan_rows(g)
                T.leave(NG)
                carried_rows()
                with dve.Fori(0, NG // 2) as i:
                    T.enter(i, LOOP_F[j])
                    for u in range(2):
                        g = i * 2 + u
                        whole_sums(g)
                        for t in range(G):
                            c = g * G + t
                            ins = STT(row_of(ys, c), row_of(ys, c), at(rcp, c), bias_row[:, j, :], ALU.mult, ALU.add)
                            if j == 1 or t < G - 1:
                                T.of(ins)
                        if j == 0:
                            ins.then_inc(f_sum[1], 1)
                            continue
                        T.wait()
                        T.step(STT(grp(xd, g), grp(ys, g), 0.0, grp(xd, g), ALU.max, ALU.add))
                        stats7(xd, g)
                        sums(st7[:], sm7[:], df7[:]).then_inc(f_sum[2], 1)
                        dve.wait_ge(f_sd[2], g + 1)
                        scales(sd7[:], sm7[:], rs7[:, u, :], nm7[:, u, :]).then_inc(f_rs[2], 1)
                T.leave(NG // 2)


_INS = ['x', 'src', 'dst', 'edge_attr_128', 'edge_type_8', 'L0_gnn_W_node', 'L0_gnn_b_node', 'L0_gnn_W_edge',
        'L0_gnn_b_edge', 'L0_gnn_W_msg', 'L0_gnn_b_msg', 'L1_gnn_W', 'L1_gnn_att_q', 'L1_gnn_att_k', 'L1_gnn_bias']


def kernel(**inputs):
    import numpy as np
    import concourse.bacc as bacc
    from concourse.bass_utils import run_bass_kernel_spmd

    nc = bacc.Bacc("TRN2", target_bir_lowering=False, num_devices=1)
    arrays, args = {}, []
    for name in _INS:
        a = np.ascontiguousarray(inputs[name])
        arrays[f"in_{name}"] = a
        args.append(nc.dram_tensor(f"in_{name}", a.shape, mybir.dt.from_np(a.dtype), kind="ExternalInput").ap())
    args.append(nc.dram_tensor("out_0", inputs["x"].shape, F32, kind="ExternalOutput").ap())
    graph_layers(nc, *args)
    r = run_bass_kernel_spmd(nc, [arrays], core_ids=[0])
    return r.results[0]["out_0"]
```

```python
from contextlib import ExitStack

import concourse.bass as bass
from concourse import mybir

ALU = mybir.AluOpType
ACT = mybir.ActivationFunctionType
AX = mybir.AxisListType
F32 = mybir.dt.float32
BF16 = mybir.dt.bfloat16
I32 = mybir.dt.int32
U8 = mybir.dt.uint8

P = 128
EPS = 1e-5
SLOPE = 0.2
BIG = 1.0e30
SKIP = 1.0e6
G = 7


class Tally:

    def __init__(self, eng, sem):
        self.eng, self.sem, self.n = eng, sem, 0

    def of(self, ins):
        ins.then_inc(self.sem, 1)
        self.n += 1
        return ins

    def wait(self, n=None):
        self.eng.wait_ge(self.sem, self.n if n is None else n)

    def step(self, ins):
        self.of(ins)
        self.wait()


def graph_layers(nc, x, src, dst, ea, typ, w_node, b_node, w_edge, b_edge, w_msg, b_msg, w_rel, att_q,
                 att_k, bias, out):
    N, D = x.shape
    E = src.shape[0]
    R = w_rel.shape[1]
    TL = -(-E // P)
    TL += -TL % G
    NG = TL // G
    EP = P * TL
    FULL = E // TL
    REST = E - FULL * TL
    assert D == P and FULL == P - 1 and 0 < REST < TL and TL <= P
    BR = 6
    BC = N // P // BR
    BREM = N - BC * BR * P
    assert BREM <= P and (N // P) % BR == 0
    SLOTS = 4
    K_A = 2
    REST_STEPS = BC + 1 - K_A - 4 * NG
    HEAD = [3, REST_STEPS - 3]
    K_H = [K_A + 2 * NG, K_A + 2 * NG + HEAD[0] + NG]
    K_M = [K_H[j] + HEAD[j] for j in range(2)]
    assert REST_STEPS >= 0 and NG % 2 == 0 and HEAD[0] >= 2
    HOLD, HELD = NG // 2 - 1, NG // 2 + 2
    GD = G * D

    x1_table = nc.dram_tensor("x1_table", (EP, D), F32).ap()
    h1_table = nc.dram_tensor("h1_table", (EP, D), F32).ap()
    src_cols = nc.dram_tensor("src_cols", (TL, P), F32).ap()
    typ_cols = nc.dram_tensor("typ_cols", (TL, P), U8).ap()

    with ExitStack() as ctx:
        def sb(name, shape, dt=F32):
            return ctx.enter_context(nc.sbuf_tensor(name, shape, dt))

        def sem(name):
            return ctx.enter_context(nc.semaphore(name))

        xs = sb("xs", [P, TL, D])
        ysz = sb("ysz", [P, TL + 1, D])
        xd = sb("xd", [P, TL, D])
        work = sb("work", [P, 2, GD])
        stage = sb("stage", [P, SLOTS * BR * D])
        mats = sb("mats", [P, TL * R])
        hot = sb("hot", [P, TL, R], U8)
        tmpk = sb("tmpk", [P, G, R])
        opT = sb("opT", [P, 2, GD])
        typB = sb("typB", [P, TL, P], U8)
        wr = sb("wr", [P, R, D])
        identS = sb("identS", [P, P + 2])
        ones = sb("ones", [P, P])
        carryF = sb("carryF", [P, P])
        carryB = sb("carryB", [P, P])
        bias_row = sb("bias_row", [P, 2, P])
        relu_row = sb("relu_row", [P, 2, P])
        turn = sb("turn", [P, P + 1])
        far = sb("far", [P, P])
        carry = turn[:, 0:P]
        wqk = sb("wqk", [P, 2, R, 2])
        qk = sb("qk", [P, 2, 2])
        bcol = sb("bcol", [P, 4])
        first = sb("first", [P, 1])
        epsc = sb("epsc", [P, 1])
        srcI = sb("srcI", [P, TL], I32)
        dstI = sb("dstI", [P, TL], I32)
        dstG = sb("dstG", [P, TL], I32)
        outI = sb("outI", [P, TL], I32)
        posI = sb("posI", [P, TL], I32)
        cols = {n: sb("c_" + n, [P, TL]) for n in
                ("same", "next", "pre", "suf", "rcp", "typ", "src1", "lg", "fm", "m", "t0")}
        colbf = sb("colbf", [P, 2, TL + 1], BF16)
        st = sb("st", [P, 2, 2 * BR, 6])
        sm = sb("sm", [P, 2, 2 * BR, 2])
        df = sb("df", [P, 2, 2 * BR])
        sd = sb("sd", [P, 2, 2 * BR])
        rs = sb("rs", [P, 2, 2 * BR])
        nm = sb("nm", [P, 2, 2 * BR])
        st7 = sb("st7", [P, G, 6])
        sm7 = sb("sm7", [P, G, 2])
        df7 = sb("df7", [P, G])
        sd7 = sb("sd7", [P, G])
        rs7 = sb("rs7", [P, 2, G])
        nm7 = sb("nm7", [P, 2, G])

        ps_y = ctx.enter_context(nc.psum_tensor("ps_y", [P, 2, 1024], F32))
        ps_t = ctx.enter_context(nc.psum_tensor("ps_t", [P, 1024], F32))
        ps_k = ctx.enter_context(nc.psum_tensor("ps_k", [P, 512], F32))
        ps_s = ctx.enter_context(nc.psum_tensor("ps_s", [P, 512], F32))

        ident = identS[:, 1:P + 1]
        ys = ysz[:, 1:TL + 1, :]
        same, nxt, pre, suf, rcp = (cols[n] for n in ("same", "next", "pre", "suf", "rcp"))
        typF, src1, lg, fm, mx, t0 = (cols[n] for n in ("typ", "src1", "lg", "fm", "m", "t0"))
        scr = xd[:, 0:16, :].rearrange("p a b -> p (a b)")
        prevI, nextI, typI, aboveI, diffI, lowI, dstF, srcF = (
            scr[:, j * P:j * P + TL].bitcast(I32) if j < 6 else scr[:, j * P:j * P + TL] for j in range(8))
        diags = scr[:, 8 * P:10 * P]
        spread = xd[:, 52:55, :].rearrange("p a b -> p (a b)")
        w_sm = scr[:, 10 * P:13 * P].rearrange("p (a b) -> p a b", a=3)
        w_mT = scr[:, 13 * P:14 * P]
        b_rep = scr[:, 14 * P:15 * P]
        bm_row = scr[:, 15 * P:16 * P]
        colsT = xd[:, 16:18, :].rearrange("p a b -> p (a b)")
        typT8 = xd[:, 18, 0:P // 4].bitcast(U8)
        wT = xd[:, 20:36, :]
        w_all = xd[:, 36:52, :]
        m_node, m_edge, c_row, sel0 = (mats[:, n * P:(n + 1) * P] for n in range(4))
        q8 = mats[:].rearrange("p (t r) -> p t r", r=R)
        srcB = work[:, 0, :]
        stepT = work[:, 1, 0:GD // 2].bitcast(BF16)
        hits = work[:, 1, GD // 2:GD // 2 + G * TL // 2].bitcast(BF16).rearrange("p (t c) -> p t c", c=TL)

        def slot(c):
            b = c % SLOTS
            return stage[:, b * BR * D:(b + 1) * BR * D].rearrange("p (r d) -> p r d", d=D)

        def grp(t, g):
            return t[:, bass.ds(g * G, G), :] if not isinstance(g, int) else t[:, g * G:g * G + G, :]

        def grpc(t, g):
            return t[:, bass.ds(g * G, G)] if not isinstance(g, int) else t[:, g * G:g * G + G]

        def row_of(t, c):
            return t[:, bass.ds(c, 1), :].rearrange("p a d -> p (a d)") if not isinstance(c, int) else t[:, c, :]

        def at(t, c):
            return t[:, bass.ds(c, 1)] if not isinstance(c, int) else t[:, c:c + 1]

        def wide(ap, n):
            return ap.unsqueeze(2).to_broadcast([ap.shape[0], ap.shape[1], n])

        def mid(ap, n):
            return ap.unsqueeze(1).to_broadcast([ap.shape[0], n, ap.shape[1]])

        idx_in = sem("idx_in"); par_in = sem("par_in"); w_diff = sem("w_diff"); ea_in = sem("ea_in"); w0_in = sem("w0_in"); w1_in = sem("w1_in")
        cols_out = sem("cols_out"); typB_in = sem("typB_in"); srcB_in = sem("srcB_in")
        bulk_in = [sem(f"bulk_in{b}") for b in range(SLOTS)]
        bulk_out = [sem(f"bulk_out{b}") for b in range(SLOTS)]
        xs_in = [[sem(f"xs_in{j}{u}") for u in range(2)] for j in range(3)]
        xd_in = [sem(f"xd_in{u}") for u in range(2)]
        tab_out = [[sem(f"tab_out{j}{u}") for u in range(2)] for j in range(2)]
        rows_out = sem("rows_out")
        consts = sem("consts"); fills = sem("fills"); idx_f = sem("idx_f"); idx_T = sem("idx_T"); idx_Tsb = sem("idx_Tsb")
        diag_r = sem("diag_r"); diag_p = sem("diag_p")
        wmT_p = sem("wmT_p"); wmT_s = sem("wmT_s"); wrT_p = sem("wrT_p"); wrT_s = sem("wrT_s")
        brep_r = sem("brep_r"); mix_p = sem("mix_p"); mix_s = sem("mix_s"); c_r = sem("c_r"); wqk_p = sem("wqk_p"); wqk_s = sem("wqk_s")
        prol_d = sem("prol_d")
        pro = sem("dve_steps")
        b_sum = sem("b_sum"); b_sd = sem("b_sd"); b_rs = sem("b_rs"); b_norm1 = sem("b_norm1"); b_norm2 = sem("b_norm2")
        a_T = sem("a_T"); a_Ts = sem("a_Ts"); a_msg = sem("a_msg"); a_ys = sem("a_ys")
        a_sum = sem("a_sum"); a_sd = sem("a_sd"); a_rs = sem("a_rs"); a_norm = sem("a_norm"); a_scan = sem("a_scan")
        p_step = sem("p_step"); p_row = sem("p_row"); p_ready = sem("p_ready")
        cy_in = sem("cy_in"); cy_ps = sem("cy_ps")
        f_sum = [sem(f"f_sum{j}") for j in range(3)]; f_sd = [sem(f"f_sd{j}") for j in range(3)]
        f_rs = [sem(f"f_rs{j}") for j in range(3)]; f_rows = [sem(f"f_rows{j}") for j in range(3)]
        f_T = [sem(f"f_T{j}") for j in range(2)]; f_Ts = [sem(f"f_Ts{j}") for j in range(2)]
        f_q = [sem(f"f_q{j}") for j in range(2)]; f_qs = [sem(f"f_qs{j}") for j in range(2)]
        m_T = [sem(f"m_T{j}") for j in range(2)]; m_Ts = [sem(f"m_Ts{j}") for j in range(2)]
        m_k = [sem(f"m_k{j}") for j in range(2)]; m_ks = [sem(f"m_ks{j}") for j in range(2)]
        m_mask = [sem(f"m_mask{j}") for j in range(2)]; m_used = [sem(f"m_used{j}") for j in range(2)]
        m_ys = [sem(f"m_ys{j}") for j in range(2)]
        s_arg = [sem(f"s_arg{j}") for j in range(2)]; s_exp = [sem(f"s_exp{j}") for j in range(2)]; s_alpha = [sem(f"s_alpha{j}") for j in range(2)]
        n_y = [sem(f"n_y{j}") for j in range(2)]
        refill = sem("refill")

        x_bulk = x[0:BC * BR * P].rearrange("(p r) d -> p r d", p=P)
        o_bulk = out[0:BC * BR * P].rearrange("(p r) d -> p r d", p=P)
        x1_rows = x1_table.rearrange("(p t) d -> p t d", p=P)
        h1_rows = h1_table.rearrange("(p t) d -> p t d", p=P)
        tables = [(x1_table, x1_rows), (h1_table, h1_rows)]

        def flat(v, a, n):
            return v[a:a + n]

        def load_cols(eng, dest, v, s):
            eng.dma_start(dest[0:FULL, :], v[0:FULL * TL].rearrange("(p t) -> p t", t=TL)).then_inc(s, 16)
            eng.dma_start(dest[FULL:P, 0:REST], v[FULL * TL:E].rearrange("(a t) -> a t", a=1)).then_inc(s, 16)

        N_IDX = 14
        N_PAR = 13

        block = ctx.enter_context(nc.Block())

        @block.sync
        def _(sp):
            load_cols(sp, srcI, src, idx_in)
            sp.dma_start(srcI[FULL:P, REST:TL], src[0:TL - REST].rearrange("(a t) -> a t", a=1)).then_inc(idx_in, 16)
            load_cols(sp, typI, typ, idx_in)
            sp.dma_start(typI[FULL:P, REST:TL], typ[0:TL - REST].rearrange("(a t) -> a t", a=1)).then_inc(idx_in, 16)
            sp.wait_ge(fills, 4)
            load_cols(sp, dstI, dst, idx_in)
            sp.dma_start(prevI[0:1, 1:TL], dst[0:TL - 1].rearrange("(a t) -> a t", a=1)).then_inc(idx_in, 16)
            sp.dma_start(prevI[1:FULL, :], dst[TL - 1:FULL * TL - 1].rearrange("(p t) -> p t", t=TL)).then_inc(idx_in, 16)
            sp.dma_start(prevI[FULL:P, 0:REST], dst[FULL * TL - 1:E - 1].rearrange("(a t) -> a t", a=1)).then_inc(idx_in, 16)
            sp.dma_start(nextI[0:FULL, :], dst[1:FULL * TL + 1].rearrange("(p t) -> p t", t=TL)).then_inc(idx_in, 16)
            sp.dma_start(nextI[FULL:P, 0:REST - 1], dst[FULL * TL + 1:E].rearrange("(a t) -> a t", a=1)).then_inc(idx_in, 16)
            sp.dma_start(aboveI[1:P, :], dst[0:FULL * TL].rearrange("(p t) -> p t", t=TL)).then_inc(idx_in, 16)
            for c in range(SLOTS):
                sp.dma_start(slot(c), x_bulk[:, c * BR:(c + 1) * BR, :]).then_inc(bulk_in[c], 16)
            sp.dma_start(w_sm[:, 0, :], w_msg).then_inc(par_in, 16)
            sp.dma_start(w_sm[:, 1, :], w_node).then_inc(par_in, 16)
            sp.dma_start(w_sm[:, 2, :], w_edge).then_inc(par_in, 16)
            sp.dma_start(bcol[:, 0:1], b_node.unsqueeze(1)).then_inc(par_in, 16)
            sp.dma_start(bcol[:, 1:2], b_edge.unsqueeze(1)).then_inc(par_in, 16)
            sp.dma_start(bm_row, b_msg.unsqueeze(0).to_broadcast([P, D])).then_inc(par_in, 16)
            sp.dma_start(bias_row[:, 0, :], bias[0:1, :].to_broadcast([P, D])).then_inc(par_in, 16)
            sp.dma_start(bias_row[:, 1, :], bias[1:2, :].to_broadcast([P, D])).then_inc(par_in, 16)
            for j in range(2):
                sp.dma_start(qk[:, j, 0:1], att_q[j]).then_inc(par_in, 16)
                sp.dma_start(qk[:, j, 1:2], att_k[j]).then_inc(par_in, 16)
            sp.dma_start(w_all, w_rel.rearrange("l r f g -> f (l r) g")).then_inc(par_in, 16)
            sp.dma_start(wr[:], w_rel[0].rearrange("r f g -> f r g")).then_inc(w0_in, 16)
            sp.dma_start(ys[0:FULL, :, :], ea[0:FULL * TL].rearrange("(p t) d -> p t d", t=TL)).then_inc(ea_in, 16)
            sp.dma_start(ys[FULL:P, 0:REST, :], ea[FULL * TL:E].unsqueeze(0)).then_inc(ea_in, 16)
            sp.dma_start(ys[FULL:P, REST:TL, :], ea[0:TL - REST].unsqueeze(0)).then_inc(ea_in, 16)
            sp.wait_ge(idx_Tsb, 2)
            sp.dma_start(src_cols, colsT[0:TL, 0:P]).then_inc(cols_out, 16)
            sp.dma_start(typ_cols, typT8[0:TL, :]).then_inc(cols_out, 16)
            sp.wait_ge(cols_out, 32)
            src_flat = src_cols.rearrange("t q -> (t q)").unsqueeze(0)
            def src_spread(g):
                part = src_flat[:, g * G * P:(g + 1) * G * P] if isinstance(g, int) else src_flat[:, bass.ds(g * (G * P), G * P)]
                sp.dma_start(srcB, part.to_broadcast([P, G * P])).then_inc(srcB_in, 16)

            src_spread(0)
            sp.dma_start(typB[:].rearrange("p t q -> p (t q)"),
                         typ_cols.rearrange("t q -> (t q)").unsqueeze(0).to_broadcast([P, EP])).then_inc(typB_in, 16)

            def bulk_step(k, kb):
                b = (kb - 1) % SLOTS
                sp.wait_ge(b_norm2, k)
                sp.dma_start(o_bulk[:, bass.ds((k - 1) * BR, BR), :] if not isinstance(k, int) else
                             o_bulk[:, (k - 1) * BR:k * BR, :], slot(b)).then_inc(bulk_out[b], 16)
                if isinstance(k, int) and k + SLOTS - 1 > BC:
                    return
                sp.wait_ge(bulk_out[b], (k - 1 - b) * (16 // SLOTS) + 16)
                if isinstance(k, int) and k + SLOTS - 1 == BC:
                    sp.dma_start(slot(b)[0:BREM, 0, :], x[BC * BR * P:N]).then_inc(bulk_in[b], 16)
                    return
                c = k + SLOTS - 1
                sp.dma_start(slot(b), x_bulk[:, bass.ds(c * BR, BR), :] if not isinstance(k, int) else
                             x_bulk[:, c * BR:(c + 1) * BR, :]).then_inc(bulk_in[b], 16)

            def bulk_steps(k0, n):
                turns = (n - SLOTS - 1) // SLOTS if k0 + n > BC - SLOTS else n // SLOTS
                with sp.Fori(0, turns) as i:
                    for q in range(SLOTS):
                        bulk_step(i * SLOTS + (k0 + q), (k0 + q) % SLOTS)
                for k in range(k0 + turns * SLOTS, k0 + n):
                    bulk_step(k, k % SLOTS)

            for k in range(1, K_A):
                bulk_step(k, k % SLOTS)
            with sp.Fori(0, NG // 2 - 1) as i:
                for u in range(2):
                    sp.wait_ge(p_step, i * 2 + (u + 1))
                    src_spread(i * 2 + (u + 1))
                    for q in range(2 * u, 2 * u + 2):
                        bulk_step(i * SLOTS + (K_A + q), (K_A + q) % SLOTS)
            sp.wait_ge(p_step, NG - 1)
            src_spread(NG - 1)
            for k in range(K_A + 2 * NG - SLOTS, K_A + 2 * NG):
                bulk_step(k, k % SLOTS)

            for j in range(2):
                rows, buf = tables[j][1], (xd, ys)[j]
                if j == 1:
                    sp.wait_ge(m_used[0], NG * (R - 1) + 2)
                    sp.dma_start(wr[:], w_rel[1].rearrange("r f g -> f r g")).then_inc(w1_in, 16)
                with sp.Fori(0, NG // 2) as i:
                    for u in range(2):
                        sp.wait_ge(f_rows[j], i * 2 + (u + 1))
                        sp.dma_start(grp(rows, i * 2 + u), grp(buf, i * 2 + u)).then_inc(tab_out[j][u], 16)
                bulk_steps(K_H[j], HEAD[j] + NG)
            sp.wait_ge(b_norm2, BC + 1)
            sp.dma_start(out[BC * BR * P:N], slot(BC)[0:BREM, 0, :]).then_inc(bulk_out[BC % SLOTS], 16)

        @block.gpsimd
        def _(pool):
            nc.gpsimd.memset(prevI, -1).then_inc(fills, 1)
            nc.gpsimd.memset(nextI, -1).then_inc(fills, 1)
            nc.gpsimd.memset(aboveI, -1).then_inc(fills, 1)
            nc.gpsimd.memset(dstI[:], N).then_inc(fills, 1)
            nc.gpsimd.memset(ones[:], 1.0).then_inc(consts, 1)
            nc.gpsimd.memset(epsc[:], EPS).then_inc(consts, 1)
            nc.gpsimd.memset(identS[:], 0.0).then_inc(consts, 1)
            nc.gpsimd.memset(sel0, 0.0).then_inc(consts, 1)
            nc.gpsimd.memset(turn[:], 0.0).then_inc(consts, 1)
            pool.wait_ge(consts, 5)
            nc.gpsimd.affine_select(out=identS[:], in_=identS[:], compare_op=ALU.not_equal, fill=1.0, base=1,
                                    pattern=[[-1, P + 2]], channel_multiplier=1).then_inc(consts, 1)
            nc.gpsimd.affine_select(out=sel0, in_=sel0, compare_op=ALU.not_equal, fill=1.0, base=0,
                                    pattern=[[0, P]], channel_multiplier=1).then_inc(consts, 1)

            def gather(buf, table, idx, sems, bound, ready=None):
                for g in range(NG):
                    u = g % 2
                    if g >= 2:
                        pool.wait_ge(sems[u], 16 * G * (g // 2))
                    if ready:
                        pool.wait_ge(ready, g + 1)
                    for t in range(g * G, g * G + G):
                        extra = {} if bound is None else dict(bounds_check=bound, oob_is_err=False)
                        nc.gpsimd.indirect_dma_start(
                            out=buf[:, t, :], out_offset=None, in_=table,
                            in_offset=bass.IndirectOffsetOnAxis(ap=idx[:, t:t + 1], axis=0), **extra).then_inc(sems[u], 16)

            pool.wait_ge(idx_in, 16 * N_IDX)
            gather(xs, x, srcI, xs_in[0], None)
            pool.wait_ge(prol_d, 1)
            pool.wait_ge(cols_out, 32)
            pool.wait_ge(mix_s, 2)
            pool.wait_ge(wqk_p, 1)
            gather(xd, x, dstG, xd_in, None)
            for j in range(2):
                pool.wait_ge(p_ready, 1)
                if j == 1:
                    for g in range(NG):
                        pool.wait_ge(m_T[0], g + 1)
                        nc.gpsimd.tensor_copy(grp(xs, g), mid(relu_row[:, 0, :], G)).then_inc(refill, 1)
                for u in range(2):
                    pool.wait_ge(tab_out[j][u], 16 * NG // 2)
                gather(xs, tables[j][0], posI, xs_in[j + 1], EP - 1, ready=(a_norm, refill)[j])
            for b in range(SLOTS):
                pool.wait_ge(bulk_out[b], 16 * len(range(b, BC + 1, SLOTS)))
            for g in range(NG):
                pool.wait_ge(f_rows[2], g + 1)
                for t in range(g * G, g * G + G):
                    nc.gpsimd.indirect_dma_start(
                        out=out, out_offset=bass.IndirectOffsetOnAxis(ap=outI[:, t:t + 1], axis=0),
                        in_=xd[:, t, :], in_offset=None, bounds_check=N - 1, oob_is_err=False).then_inc(rows_out, 16)
            pool.wait_ge(rows_out, 16 * TL)

        @block.tensor
        def _(pe):
            pe.wait_ge(consts, 7)
            pe.wait_ge(idx_f, 1)
            pe.transpose(ps_s[0:TL, 0:P], srcF, ident)
            pe.transpose(ps_s[0:TL, P:2 * P], typF[:], ident).then_inc(idx_T, 1)
            pe.wait_ge(par_in, 16 * N_PAR)
            pe.transpose(ps_t[:, 0:P], w_sm[:, 0, :], ident).then_inc(wmT_p, 1)
            for a in range(2 * R):
                mm = pe.transpose(ps_y[:, a // R, a % R * P:(a % R + 1) * P], w_all[:, a, :], ident)
            mm.then_inc(wrT_p, 1)
            pe.wait_ge(diag_r, 1)
            pe.wait_ge(idx_Tsb, 2)
            pe.matmul(ps_s[:, 2 * P:4 * P], ones[:], diags, start=True, stop=True).then_inc(diag_p, 1)
            pe.wait_ge(wmT_s, 1)
            pe.matmul(ps_t[:, P:2 * P], w_sm[:, 1, :], w_mT, start=True, stop=True)
            pe.matmul(ps_t[:, 2 * P:3 * P], w_sm[:, 2, :], w_mT, start=True, stop=True)
            pe.wait_ge(brep_r, 1)
            pe.matmul(ps_t[:, 3 * P:4 * P], b_rep, w_mT, start=True, stop=True).then_inc(mix_p, 1)
            pe.wait_ge(wrT_s, 1)
            for a in range(2 * R):
                mm = pe.matmul(ps_k[:, 2 * a:2 * a + 2], wT[:, a, :], qk[:, a // R, :], start=True, stop=True)
            mm.then_inc(wqk_p, 1)

            pe.wait_ge(mix_s, 2)
            pe.wait_ge(c_r, 1)
            pe.wait_ge(ea_in, 48)
            for g in range(NG):
                pe.wait_ge(p_step, g + 1)
                for t in range(G):
                    o = ps_y[:, 1, t * P:t * P + TL + 1]
                    pe.matmul(o, stepT[:, t * P:(t + 1) * P], colbf[:, 0, :], start=True, stop=False)
                    mm = pe.matmul(o, stepT[:, t * P:(t + 1) * P], colbf[:, 1, :], start=False, stop=True)
                mm.then_inc(p_row, 1)
                u = g % 2
                pe.wait_ge(xs_in[0][u], (g // 2 + 1) * (16 * G))
                pe.wait_ge(a_Ts, g * 2 + 1)
                for t in range(G):
                    mm = pe.transpose(ps_t[:, t * P:(t + 1) * P], row_of(xs, g * G + t), ident)
                mm.then_inc(a_T, 1)
                pe.wait_ge(a_Ts, g * 2 + 2)
                for t in range(G):
                    mm = pe.transpose(ps_t[:, t * P:(t + 1) * P], row_of(ys, g * G + t), ident)
                mm.then_inc(a_T, 1)
                pe.wait_ge(a_Ts, g * 2 + 3)
                pe.wait_ge(a_ys, g + 1)
                for t in range(G):
                    o = ps_y[:, 0, t * P:(t + 1) * P]
                    pe.matmul(o, opT[:, 0, t * P:(t + 1) * P], m_node, start=True, stop=False)
                    pe.matmul(o, opT[:, 1, t * P:(t + 1) * P], m_edge, start=False, stop=False)
                    mm = pe.matmul(o, sel0, c_row, start=False, stop=True)
                mm.then_inc(a_msg, 1)

            uses = [0]

            def carry_product(mat, rhs, n):
                uses[0] += 1
                pe.wait_ge(cy_in, uses[0])
                pe.matmul(ps_s[:, 0:n], mat, rhs, start=True, stop=True).then_inc(cy_ps, 1)

            def carry_turn():
                uses[0] += 1
                pe.wait_ge(cy_in, uses[0])
                pe.transpose(ps_s[:, 0:P], turn[:, 0:P], ident).then_inc(cy_ps, 1)

            def node_scores(j):
                buf = (xd, ys)[j]
                for g in range(NG):
                    u = g % 2
                    pe.wait_ge(f_rows[j], g + 1)
                    pe.wait_ge(f_Ts[j], g + 1)
                    for t in range(G):
                        mm = pe.transpose(ps_t[:, t * P:(t + 1) * P], row_of(buf, g * G + t), ident)
                    mm.then_inc(f_T[j], 1)
                    pe.wait_ge(f_Ts[j], g + 2)
                    pe.wait_ge(f_qs[j], g + 1)
                    for t in range(G):
                        mm = pe.matmul(ps_k[:, t * R:(t + 1) * R], opT[:, u, t * P:(t + 1) * P], wqk[:, j, :, 0],
                                       start=True, stop=True)
                    mm.then_inc(f_q[j], 1)

            def relation_products(j):
                pe.wait_ge(w_diff, j + 1)

                def turn_rows(g, u, rows_in):
                    pe.wait_ge(xs_in[j + 1][u], rows_in)
                    pe.wait_ge(m_Ts[j], g + 1)
                    for t in range(G):
                        mm = pe.transpose(ps_t[:, t * P:(t + 1) * P], row_of(xs, g * G + t), ident)
                    mm.then_inc(m_T[j], 1)

                def key_scores(g, u):
                    pe.wait_ge(m_Ts[j], g + 2)
                    pe.wait_ge(m_ks[j], g + 1)
                    for t in range(G):
                        mm = pe.matmul(ps_k[:, t * R:(t + 1) * R], opT[:, u, t * P:(t + 1) * P],
                                       wqk[:, j, :, 1], start=True, stop=True)
                    mm.then_inc(m_k[j], 1)

                def products(g, u):
                    pe.wait_ge(m_ys[j], g + 1)
                    for r in range(R):
                        n = g * (R - 1) + r - 1
                        if r:
                            pe.wait_ge(m_mask[j], n + 1 + 2 * (R - 1))
                        for t in range(G):
                            rows = (work[:, n % 2, :] if r else opT[:, u, :])[:, t * P:(t + 1) * P]
                            mm = pe.matmul(ps_y[:, u, t * P:(t + 1) * P], rows, wr[:, r, :],
                                           start=(r == 0 and t % 4 == 0), stop=(r == R - 1),
                                           skip_group_check=True)
                        if r:
                            mm.then_inc(m_used[j], 1)

                pe.sem_inc(m_used[j], 2)
                turn_rows(0, 0, 16 * G)
                key_scores(0, 0)
                for g in range(NG):
                    u = g % 2
                    if g < NG - 1:
                        turn_rows(g + 1, 1 - u, ((g + 1) // 2 + 1) * (16 * G))
                    products(g, u)
                    if g < NG - 1:
                        key_scores(g + 1, 1 - u)
                    if g == HELD - 1:
                        carry_product(carryB[:], q8[:, 0, :], R)

            carry_product(carryF[:], t0[:, TL - 1:TL], 1)
            carry_product(carryF[:], ys[:, TL - 1, :], P)
            node_scores(0)
            for j in range(2):
                relation_products(j)
                carry_turn()
                carry_turn()
                carry_product(carryB[:], mx[:, 0:1], 1)
                carry_product(carryF[:], fm[:, TL - 1:TL], 1)
                carry_product(carryB[:], rcp[:, 0:1], 1)
                carry_product(carryF[:], ys[:, TL - 1, :], P)
                if j == 0:
                    node_scores(1)

        @block.scalar
        def _(act):
            a = nc.scalar

            def copy(o, i_):
                return a.activation(o, i_, ACT.Copy)

            act.sem_inc(a_Ts, 1)
            act.sem_inc(a_ys, 1)
            for j in range(2):
                act.sem_inc(f_qs[j], 1)
                act.sem_inc(f_Ts[j], 1)
                act.sem_inc(m_Ts[j], 1)
                act.sem_inc(m_ys[j], 2)
            act.wait_ge(idx_T, 1)
            copy(colsT[0:TL, 0:P], ps_s[0:TL, 0:P]).then_inc(idx_Tsb, 1)
            copy(typT8[0:TL, :], ps_s[0:TL, P:2 * P]).then_inc(idx_Tsb, 1)
            act.wait_ge(wmT_p, 1)
            copy(w_mT, ps_t[:, 0:P]).then_inc(wmT_s, 1)
            act.wait_ge(wrT_p, 1)
            copy(wT[:, 0:R, :], ps_y[:, 0, :].rearrange("p (a b) -> p a b", b=P))
            copy(wT[:, R:2 * R, :], ps_y[:, 1, :].rearrange("p (a b) -> p a b", b=P)).then_inc(wrT_s, 1)
            act.wait_ge(mix_p, 1)
            copy(m_node, ps_t[:, P:2 * P]).then_inc(mix_s, 1)
            copy(m_edge, ps_t[:, 2 * P:3 * P]).then_inc(mix_s, 1)
            act.wait_ge(wqk_p, 1)
            copy(wqk[:].rearrange("p l r a -> p (l r a)"), ps_k[:, 0:4 * R]).then_inc(wqk_s, 1)

            def bulk_sd(k, kb, first=True, second=True):
                h, lo, hi = kb % 2, 0 if first else BR, 2 * BR if second else BR
                act.wait_ge(b_sum, k + 1)
                a.activation(sd[:, h, lo:hi], df[:, h, lo:hi], ACT.Sqrt, bias=epsc[:, 0:1], scale=1.0 / D).then_inc(b_sd, 1)

            def bulk_norms(k, kb, first=True, second=True):
                h = kb % 2
                act.wait_ge(b_rs, k + 1)
                for half, c, s_ in ((0, kb, b_norm1), (1, kb - 1, b_norm2)):
                    if not (first, second)[half]:
                        continue
                    for r in range(BR):
                        n = half * BR + r
                        ins = a.activation(slot(c)[:, r, :], slot(c)[:, r, :], ACT.Identity,
                                           bias=nm[:, h, n:n + 1], scale=rs[:, h, n:n + 1])
                    ins.then_inc(s_, 1)

            def bulk_step(k, kb, first=True, second=True):
                bulk_sd(k, kb, first, second)
                bulk_norms(k, kb, first, second)

            def out_of_psum(o, i_, producer, n, done):
                act.wait_ge(producer, n)
                copy(o, i_).then_inc(done, 1)

            bulk_step(0, 0, second=False)
            for k in range(1, K_A):
                bulk_step(k, k % SLOTS)
            for i in range(NG // 2):
                for u in range(2):
                    g = i * 2 + u
                    kA, kB = (i * SLOTS + (K_A + 2 * u + q) for q in range(2))
                    bA, bB = ((K_A + 2 * u + q) % SLOTS for q in range(2))
                    out_of_psum(opT[:, 0, :], ps_t[:, 0:GD], a_T, g * 2 + 1, a_Ts)
                    bulk_sd(kA, bA)
                    out_of_psum(opT[:, 1, :], ps_t[:, 0:GD], a_T, g * 2 + 2, a_Ts)
                    act.wait_ge(a_sum, g + 1)
                    a.activation(sd7[:], df7[:], ACT.Sqrt, bias=epsc[:, 0:1], scale=1.0 / D).then_inc(a_sd, 1)
                    bulk_norms(kA, bA)
                    act.wait_ge(a_rs, g + 1)
                    for t in range(G):
                        ins = a.activation(row_of(xs, g * G + t), row_of(xs, g * G + t), ACT.Identity,
                                           bias=nm7[:, u, t:t + 1], scale=rs7[:, u, t:t + 1])
                    ins.then_inc(a_norm, 1)
                    bulk_sd(kB, bB)
                    out_of_psum(grp(ys, g).rearrange("p a b -> p (a b)"), ps_y[:, 0, 0:GD], a_msg, g + 1, a_ys)
                    bulk_norms(kB, bB)

            def query_rows_out(j, g, u):
                out_of_psum(opT[:, u, :], ps_t[:, 0:GD], f_T[j], g + 1, f_Ts[j])

            def query_scores_out(j, g):
                out_of_psum(grp(q8, g), ps_k[:, 0:G * R].rearrange("p (t r) -> p t r", r=R), f_q[j], g + 1, f_qs[j])

            def norm_rows(j, g, u, last=None):
                act.wait_ge(f_sum[j], g + 1)
                a.activation(sd7[:], df7[:], ACT.Sqrt, bias=epsc[:, 0:1], scale=1.0 / D).then_inc(f_sd[j], 1)
                act.wait_ge(f_rs[j], g + 1)
                for t in range(G):
                    ins = a.activation(row_of(xd, g * G + t), row_of(xd, g * G + t), ACT.Identity,
                                       bias=nm7[:, u, t:t + 1], scale=rs7[:, u, t:t + 1])
                ins.then_inc(f_rows[j], 1)
                if last is not None:
                    query_rows_out(j, last, 1 - u)
                if last:
                    query_scores_out(j, last - 1)

            for g in range(NG):
                norm_rows(0, g, g % 2, last=g - 1 if g else None)
            bulk_step(K_H[0], K_H[0] % SLOTS)
            query_rows_out(0, NG - 1, 1)
            query_scores_out(0, NG - 2)
            bulk_step(K_H[0] + 1, (K_H[0] + 1) % SLOTS)
            query_scores_out(0, NG - 1)

            for j in range(2):
                def rows_T(g, u):
                    act.wait_ge(m_mask[j], (g + 1) * (R - 1))
                    out_of_psum(opT[:, u, :], ps_t[:, 0:GD], m_T[j], g + 1, m_Ts[j])

                def products_out(g, u):
                    out_of_psum(grp(ys, g).rearrange("p a b -> p (a b)"), ps_y[:, u, 0:GD],
                                m_used[j], (g + 1) * (R - 1) + 2, m_ys[j])

                def group(g, q, k):
                    rows_T(g + 1, (q + 1) % 2)
                    bulk_step(k, (K_M[j] + q) % SLOTS)
                    products_out(g, q % 2)

                if j == 0:
                    for k in range(K_H[0] + 2, K_M[0]):
                        bulk_step(k, k % SLOTS)
                rows_T(0, 0)
                for i in range(NG // SLOTS):
                    for q in range(SLOTS):
                        group(i * SLOTS + q, q, i * SLOTS + (K_M[j] + q))
                for g in range(NG // SLOTS * SLOTS, NG - 1):
                    group(g, g % SLOTS, K_M[j] + g)
                bulk_step(K_M[j] + NG - 1, (K_M[j] + NG - 1) % SLOTS)
                products_out(NG - 1, 1)
                if j == 1:
                    bulk_step(BC + 1, (BC + 1) % SLOTS, first=False)
                act.wait_ge(s_arg[j], 1)
                a.activation(lg[:], lg[:], ACT.Exp).then_inc(s_exp[j], 1)
                act.wait_ge(s_alpha[j], 1)
                act.wait_ge(m_ys[j], NG + 2)
                for g in range(NG):
                    for t in range(G):
                        ins = a.activation(row_of(ys, g * G + t), row_of(ys, g * G + t), ACT.Copy, scale=at(lg, g * G + t))
                    ins.then_inc(n_y[j], 1)
                if j == 0:
                    for g in range(NG):
                        act.wait_ge(f_sum[1], g + 1)
                        a.activation(grp(ys, g), grp(ys, g), ACT.Relu).then_inc(f_rows[1], 1)
                        if g % 3 and g < NG - 1:
                            n = g // 3 * 2 + g % 3 - 1
                            query_rows_out(1, n, n % 2)
                            if n:
                                query_scores_out(1, n - 1)
                    k = K_H[1]
                    for m in range(n + 1, NG):
                        if k < K_M[1]:
                            bulk_step(k, k % SLOTS)
                            k += 1
                        query_rows_out(1, m, m % 2)
                        query_scores_out(1, m - 1)
                    query_scores_out(1, NG - 1)
                    for k in range(k, K_M[1]):
                        bulk_step(k, k % SLOTS)
                else:
                    for i in range(NG // 2):
                        for u in range(2):
                            norm_rows(2, i * 2 + u, u)

        @block.vector
        def _(dve):
            v = nc.vector
            T = Tally(dve, pro)
            STT, TT, TS = v.scalar_tensor_tensor, v.tensor_tensor, v.tensor_scalar

            for j in range(2):
                dve.sem_inc(m_mask[j], 2 * (R - 1))
                dve.sem_inc(m_ks[j], 1)
            dve.wait_ge(idx_in, 16 * N_IDX)
            T.of(v.tensor_copy(srcF, srcI[:]))
            T.of(v.tensor_copy(typF[:], typI))
            T.of(v.tensor_copy(dstF, dstI[:]))
            T.of(v.tensor_copy(first[:], dstI[:, 0:1]))
            T.of(TT(same[:], dstI[:], prevI, ALU.is_equal))
            T.of(TT(nxt[:], dstI[:], nextI, ALU.is_equal))
            T.of(TS(dstG[:], dstI[:], float(N - 1), None, ALU.min))
            T.step(TT(diffI, dstI[:], aboveI, ALU.subtract))
            T.step(TS(src1[:], srcF, 1.0, None, ALU.add))
            dve.sem_inc(idx_f, 1)
            T.of(v.tensor_tensor_scan(pre[:], same[:], same[:], 1.0, ALU.mult, ALU.min))
            T.of(v.tensor_tensor_scan(suf[:, ::-1], nxt[:, ::-1], nxt[:, ::-1], 1.0, ALU.mult, ALU.min))
            T.of(STT(t0[:], nxt[:], SKIP, dstF, ALU.mult, ALU.add))
            T.of(TS(lowI, diffI, 255, None, ALU.bitwise_and))
            T.step(v.memset(colbf[:, 0, TL:TL + 1], 1.0))
            T.of(v.memset(colbf[:, 1, TL:TL + 1], 0.0))
            T.of(v.tensor_copy(outI[:], t0[:]))
            T.of(TT(colbf[:, 0, 0:TL], diffI, lowI, ALU.subtract))
            T.of(v.tensor_copy(colbf[:, 1, 0:TL], lowI))
            dve.wait_ge(consts, 7)
            T.of(TS(diags[:, 0:P], ident, pre[:, TL - 1:TL], None, ALU.mult))
            T.step(TS(diags[:, P:2 * P], ident, suf[:, 0:1], None, ALU.mult))
            dve.sem_inc(diag_r, 1)
            dve.wait_ge(par_in, 16 * N_PAR)
            T.step(TT(bcol[:, 2:3], bcol[:, 0:1], bcol[:, 1:2], ALU.add))
            T.of(TS(relu_row[:], bias_row[:], 0.0, None, ALU.max))
            T.step(TS(b_rep, ones[:], bcol[:, 2:3], None, ALU.mult))
            dve.sem_inc(brep_r, 1)
            dve.wait_ge(diag_p, 1)
            T.of(v.memset(spread[:, 0:1], 0.0))
            T.of(v.memset(spread[:, 2 * P + 1:2 * P + 2], 0.0))
            T.of(v.tensor_copy(spread[:, 1:2 * P + 1], ps_s[:, 2 * P:4 * P]))
            T.step(TS(far[0:1, :], ps_s[0:1, 2 * P:3 * P], 1.0, BIG, ALU.subtract, ALU.mult))
            T.of(v.tensor_tensor_scan(carryF[:], spread[:, 0:P], identS[:, 0:P], 0.0, ALU.mult, ALU.add))
            T.step(v.tensor_tensor_scan(carryB[:, ::-1], spread[:, P + 2:2 * P + 2][:, ::-1], identS[:, 2:P + 2][:, ::-1],
                                        0.0, ALU.mult, ALU.add))
            dve.wait_ge(mix_s, 2)
            T.step(TT(c_row, ps_t[:, 3 * P:4 * P], bm_row, ALU.add))
            dve.sem_inc(c_r, 1)
            dve.sem_inc(prol_d, 1)

            def sums(stats, s2, d):
                T.of(TT(s2, stats[:, :, 1:3], stats[:, :, 4:6], ALU.add))
                T.step(TT(d, stats[:, :, 1], stats[:, :, 4], ALU.subtract))
                T.step(STT(d, d, 32.0, d, ALU.mult, ALU.mult))
                return TT(d, d, s2[:, :, 1], ALU.add)

            def scales(dev, s2, r_, n_):
                T.step(v.reciprocal(r_, dev))
                return STT(n_, s2[:, :, 0], -0.5, r_, ALU.mult, ALU.mult)

            def bulk_first(k, kb, rows=range(BR)):
                dve.wait_ge(bulk_in[kb], (k - kb) * (16 // SLOTS) + 16)
                for r in rows:
                    T.of(v.bn_stats(st[:, kb % 2, r, :], slot(kb)[:, r, :]))

            def bulk_shift(k, kb):
                dve.wait_ge(b_norm1, k)
                T.of(TT(slot(kb - 1), slot(kb - 1), mid(relu_row[:, 1, :], BR), ALU.add))

            def bulk_second(k, kb, rows=range(BR)):
                for r in rows:
                    if r == 0:
                        T.wait()
                    T.of(v.bn_stats(st[:, kb % 2, BR + r, :], slot(kb - 1)[:, r, :]))

            def bulk_sums(k, kb, lo=0, hi=2 * BR):
                h = kb % 2
                T.wait()
                sums(st[:, h, lo:hi, :], sm[:, h, lo:hi, :], df[:, h, lo:hi]).then_inc(b_sum, 1)

            def bulk_scales(k, kb, lo=0, hi=2 * BR):
                h = kb % 2
                dve.wait_ge(b_sd, k + 1)
                scales(sd[:, h, lo:hi], sm[:, h, lo:hi, :], rs[:, h, lo:hi], nm[:, h, lo:hi]).then_inc(b_rs, 1)

            def bulk_statistics(k, kb, first=True, second=True):
                if first:
                    bulk_first(k, kb)
                if second:
                    bulk_shift(k, kb)
                    bulk_second(k, kb)
                bulk_sums(k, kb, 0 if first else BR, 2 * BR if second else BR)

            def bulk_step(k, kb, first=True, second=True):
                bulk_statistics(k, kb, first, second)
                bulk_scales(k, kb, 0 if first else BR, 2 * BR if second else BR)

            def bulk_piece(n, k, kb):
                if n < 2:
                    bulk_first(k, kb, range(n * BR // 2, (n + 1) * BR // 2))
                elif n == 2:
                    bulk_shift(k, kb)
                elif n < 5:
                    bulk_second(k, kb, range((n - 3) * BR // 2, (n - 2) * BR // 2))
                elif n == 5:
                    bulk_sums(k, kb)
                elif n == 7:
                    bulk_scales(k, kb)

            def scan_rows(g, between=lambda t: None):
                for t in range(G):
                    c = g * G + t
                    T.of(STT(row_of(ys, c), row_of(ysz, c), at(same, c), row_of(ys, c), ALU.mult, ALU.add))
                    summed = T.n
                    between(t)
                    T.wait(summed)

            def stats7(buf, g):
                for t in range(G):
                    T.of(v.bn_stats(st7[:, t, :], row_of(buf, g * G + t)))
                T.wait()

            T.step(v.memset(ysz[:, 0, :], 0.0))
            bulk_step(0, 0, second=False)
            for k in range(1, K_A):
                bulk_step(k, k % SLOTS)

            def search(g, between):
                dve.wait_ge(p_row, g + 1)
                rows = ps_y[:, 1, :].rearrange("p (t c) -> p t c", c=P)[:, 0:G, :]
                mine = wide(grpc(src1, g), TL)
                T.of(TS(grpc(mx, g), rows[:, :, TL], float(TL), None, ALU.mult))
                for n, (op, o, red) in enumerate(((ALU.is_le, fm, ALU.add), (ALU.is_equal, lg, ALU.max))):
                    T.of(TT(hits, rows[:, :, 0:TL], mine, op))
                    found = T.n
                    between(2 * n)
                    T.wait(found)
                    T.of(v.tensor_reduce(grpc(o, g), hits, AX.X, red))
                    found = T.n
                    between(2 * n + 1)
                    T.wait(found)

            def spread_steps(g):
                dve.wait_ge(srcB_in, 16 * (g + 1))
                TS(stepT, srcB, first[:, 0:1], None, ALU.is_ge).then_inc(p_step, 1)

            for r in range(R):
                T.of(TS(hot[:, :, r], typF[:], float(r), None, ALU.is_equal))
            spread_steps(0)
            for g in range(NG):
                u = g % 2
                kA, kB = (K_A + 2 * g + q for q in range(2))
                bA, bB = kA % SLOTS, kB % SLOTS
                if g:
                    dve.wait_ge(a_ys, g + 1)
                    scan_rows(g - 1, lambda t: bulk_first(kA, bA, range(t, t + 1)) if t < BR else None)
                else:
                    bulk_first(kA, bA)
                bulk_shift(kA, bA)
                bulk_second(kA, bA)
                bulk_sums(kA, bA)
                dve.wait_ge(xs_in[0][u], g // 2 * (16 * G) + 16 * G)
                stats7(xs, g)
                sums(st7[:], sm7[:], df7[:]).then_inc(a_sum, 1)
                bulk_scales(kA, bA)
                search(g, lambda n: bulk_first(kB, bB, range(n, n + 1)))
                dve.wait_ge(a_sd, g + 1)
                scales(sd7[:], sm7[:], rs7[:, u, :], nm7[:, u, :]).then_inc(a_rs, 1)
                bulk_first(kB, bB, range(4, BR))
                bulk_shift(kB, bB)
                bulk_second(kB, bB)
                bulk_sums(kB, bB)
                if g < NG - 1:
                    spread_steps(g + 1)
                bulk_scales(kB, bB)
            dve.wait_ge(a_ys, NG + 1)
            scan_rows(NG - 1)
            T.step(TT(fm[:], fm[:], mx[:], ALU.add))
            T.step(TS(lg[:], lg[:], -SKIP, SKIP - TL - 1.0, ALU.mult, ALU.add))
            T.step(TT(lg[:], lg[:], fm[:], ALU.add))
            T.step(v.tensor_copy(posI[:], lg[:]))
            dve.sem_inc(p_ready, 1)

            uses = [0]

            def hand_over():
                uses[0] += 1
                dve.sem_inc(cy_in, 1)

            def take():
                dve.wait_ge(cy_ps, uses[0])

            def carried():
                hand_over()
                take()

            def carried_rows():
                carried()
                T.step(v.tensor_copy(carry, ps_s[:, 0:P]))

            T.step(v.tensor_tensor_scan(t0[:], same[:], ones[:, 0:TL], 0.0, ALU.mult, ALU.add))
            carried()
            T.step(STT(t0[:], pre[:], ps_s[:, 0:1], t0[:], ALU.mult, ALU.add))
            T.step(v.reciprocal(rcp[:], t0[:]))
            carried_rows()

            def whole_sums(g):
                for t in range(G):
                    c = g * G + t
                    T.of(STT(row_of(ys, c), carry, at(pre, c), row_of(ys, c), ALU.mult, ALU.add))
                T.wait()

            def row_scales(j, g):
                dve.wait_ge(f_sd[j], g + 1)
                scales(sd7[:], sm7[:], rs7[:, g % 2, :], nm7[:, g % 2, :]).then_inc(f_rs[j], 1)

            for g in range(NG):
                whole_sums(g)
                dve.wait_ge(xd_in[g % 2], (g // 2 + 1) * (16 * G))
                for t in range(G):
                    c = g * G + t
                    T.of(STT(row_of(xd, c), row_of(ys, c), at(rcp, c), row_of(xd, c), ALU.mult, ALU.add))
                if g:
                    row_scales(0, g - 1)
                T.wait()
                stats7(xd, g)
                sums(st7[:], sm7[:], df7[:]).then_inc(f_sum[0], 1)
            row_scales(0, NG - 1)

            for j in range(2):
                for k in range(K_H[j], K_M[j]):
                    bulk_step(k, k % SLOTS)
                dve.wait_ge((w0_in, w1_in)[j], 16)
                T.step(TT(wr[:, 1:R, :], wr[:, 1:R, :], mid(wr[:, 0, :], R - 1), ALU.subtract))
                dve.sem_inc(w_diff, 1)
                if j == 0:
                    dve.wait_ge(typB_in, 16)

                def hold_queries():
                    dve.wait_ge(f_qs[j], NG + 1)
                    T.step(TS(t0[:], nxt[:], -1.0, 1.0, ALU.mult, ALU.add))
                    T.step(TT(q8, q8, wide(t0[:], R), ALU.mult))
                    for r in range(R):
                        T.of(v.tensor_tensor_scan(q8[:, ::-1, r], nxt[:, ::-1], q8[:, ::-1, r], 0.0, ALU.mult, ALU.add))
                    T.wait()
                    hand_over()

                def held_queries():
                    take()
                    for r in range(R):
                        T.of(STT(q8[:, :, r], suf[:], ps_s[:, r:r + 1], q8[:, :, r], ALU.mult, ALU.add))

                def group(g, q, k):
                    dve.wait_ge(m_Ts[j], g + 2)
                    bulk_piece(0, k, k % SLOTS)
                    for r in range(1, R):
                        n = g * (R - 1) + r - 1
                        dve.wait_ge(m_used[j], n + 1)
                        STT(work[:, n % 2, :], grp(typB, g).rearrange("p a b -> p (a b)"), float(r),
                            opT[:, q % 2, :], ALU.is_equal, ALU.mult).then_inc(m_mask[j], 1)
                        bulk_piece(r, k, k % SLOTS)
                    dve.wait_ge(m_k[j], g + 1)
                    TT(tmpk[:], ps_k[:, 0:G * R].rearrange("p (t r) -> p t r", r=R), grp(hot, g), ALU.mult).then_inc(m_ks[j], 1)
                    dve.wait_ge(m_ks[j], g + 2)
                    T.step(v.tensor_reduce(grpc(lg, g), tmpk[:], AX.X, ALU.add))
                    if g == HOLD:
                        hold_queries()
                    if g == HELD:
                        held_queries()

                for i in range(NG // SLOTS):
                    for q in range(SLOTS):
                        group(i * SLOTS + q, q, i * SLOTS + (K_M[j] + q))
                for g in range(NG // SLOTS * SLOTS, NG):
                    group(g, g % SLOTS, K_M[j] + g)
                if j == 1:
                    bulk_step(BC + 1, (BC + 1) % SLOTS, first=False)
                T.step(TT(q8, q8, hot[:], ALU.mult))
                T.step(v.tensor_reduce(t0[:], q8, AX.X, ALU.add))
                T.step(TT(t0[:], t0[:], lg[:], ALU.add))
                T.step(STT(lg[:], t0[:], SLOPE, t0[:], ALU.mult, ALU.max))
                T.step(TS(t0[:], same[:], 1.0, BIG, ALU.subtract, ALU.mult))
                T.step(v.tensor_tensor_scan(fm[:], t0[:], lg[:], -BIG, ALU.add, ALU.max))
                T.step(v.tensor_copy(turn[:, 0:1], fm[:, TL - 1:TL]))
                carried()
                T.of(v.tensor_tensor_scan(turn[0:1, 1:P + 1], far[0:1, :], ps_s[0:1, 0:P], -BIG, ALU.add, ALU.max))
                T.step(v.memset(turn[0:1, 0:1], -BIG))
                carried()
                T.step(v.tensor_copy(mx[:, 0:1], ps_s[:, 0:1]))
                T.step(v.tensor_tensor_scan(fm[:], t0[:], lg[:], mx[:, 0:1], ALU.add, ALU.max))
                T.step(TT(t0[:], nxt[:], fm[:], ALU.mult))
                T.step(TT(t0[:], fm[:], t0[:], ALU.subtract))
                T.step(v.tensor_tensor_scan(mx[:, ::-1], nxt[:, ::-1], t0[:, ::-1], 0.0, ALU.mult, ALU.add))
                carried()
                T.step(STT(mx[:], suf[:], ps_s[:, 0:1], mx[:], ALU.mult, ALU.add))
                T.step(TT(lg[:], lg[:], mx[:], ALU.subtract))
                dve.sem_inc(s_arg[j], 1)
                dve.wait_ge(s_exp[j], 1)
                T.step(v.tensor_tensor_scan(fm[:], same[:], lg[:], 0.0, ALU.mult, ALU.add))
                carried()
                T.step(STT(fm[:], pre[:], ps_s[:, 0:1], fm[:], ALU.mult, ALU.add))
                T.step(TT(t0[:], nxt[:], fm[:], ALU.mult))
                T.step(TT(t0[:], fm[:], t0[:], ALU.subtract))
                T.step(v.tensor_tensor_scan(rcp[:, ::-1], nxt[:, ::-1], t0[:, ::-1], 0.0, ALU.mult, ALU.add))
                carried()
                T.step(STT(rcp[:], suf[:], ps_s[:, 0:1], rcp[:], ALU.mult, ALU.add))
                T.step(TS(rcp[:], rcp[:], 1e-16, None, ALU.add))
                T.step(v.reciprocal(rcp[:], rcp[:]))
                T.step(TT(lg[:], lg[:], rcp[:], ALU.mult))
                dve.sem_inc(s_alpha[j], 1)
                for g in range(NG):
                    dve.wait_ge(n_y[j], g + 1)
                    scan_rows(g)
                carried_rows()
                for g in range(NG):
                    whole_sums(g)
                    ins = TT(grp(ys, g), grp(ys, g), mid(bias_row[:, j, :], G), ALU.add)
                    if j == 0:
                        ins.then_inc(f_sum[1], 1)
                        continue
                    T.of(ins)
                    if g:
                        row_scales(2, g - 1)
                    T.wait()
                    T.step(STT(grp(xd, g), grp(ys, g), 0.0, grp(xd, g), ALU.max, ALU.add))
                    stats7(xd, g)
                    sums(st7[:], sm7[:], df7[:]).then_inc(f_sum[2], 1)
                if j == 1:
                    row_scales(2, NG - 1)


_INS = ['x', 'src', 'dst', 'edge_attr_128', 'edge_type_8', 'L0_gnn_W_node', 'L0_gnn_b_node', 'L0_gnn_W_edge',
        'L0_gnn_b_edge', 'L0_gnn_W_msg', 'L0_gnn_b_msg', 'L1_gnn_W', 'L1_gnn_att_q', 'L1_gnn_att_k', 'L1_gnn_bias']


def kernel(**inputs):
    import numpy as np
    import concourse.bacc as bacc
    from concourse.bass_utils import run_bass_kernel_spmd

    nc = bacc.Bacc("TRN2", target_bir_lowering=False, num_devices=1)
    arrays, args = {}, []
    for name in _INS:
        a = np.ascontiguousarray(inputs[name])
        arrays[f"in_{name}"] = a
        args.append(nc.dram_tensor(f"in_{name}", a.shape, mybir.dt.from_np(a.dtype), kind="ExternalInput").ap())
    args.append(nc.dram_tensor("out_0", inputs["x"].shape, F32, kind="ExternalOutput").ap())
    graph_layers(nc, *args)
    r = run_bass_kernel_spmd(nc, [arrays], core_ids=[0])
    return r.results[0]["out_0"]
```
